# Optimizing a Trainium2 kernel written in Bass

```python
import numpy as np
import jax
import jax.numpy as jnp

def _softmax(x, axis=-1):
    return jax.nn.softmax(x, axis=axis)

def _gelu(x):
    return jax.nn.gelu(x, approximate=True)

def _silu(x):
    return jax.nn.silu(x)

def _sigmoid(x):
    return jax.nn.sigmoid(x)

def _layernorm(x, axis=-1, eps=1e-05):
    m = jnp.mean(x, axis=axis, keepdims=True)
    v = jnp.var(x, axis=axis, keepdims=True)
    return (x - m) / jnp.sqrt(v + eps)

def _scatter_add(tgt, idx, src, axis=0):
    return tgt.at[idx].add(src)

def _segment_sum(src, seg, n):
    return jax.ops.segment_sum(src, seg, n)
kernel_name = 'mk_flamingo_gated_d1_seqx_r4_e62d9c'

def setup_inputs(seed: int=0):
    np.random.seed(seed)
    _w = jnp.asarray

    def _rec_inputs():
        import jax
        import jax.numpy as jnp
        _rk = jax.random.key(seed)
        x = -0.000125 + 0.9999 * jax.random.normal(jax.random.fold_in(_rk, 1), (32, 128, 256), jnp.float32)
        _lenS = 128 - jax.random.randint(jax.random.fold_in(_rk, 7), (32,), 0, max(1, 128 // 4) + 1, jnp.int32)
        _lenS2 = 128 - jax.random.randint(jax.random.fold_in(_rk, 8), (32,), 0, max(1, 128 // 4) + 1, jnp.int32)
        _ctx_1024P = jax.random.normal(jax.random.fold_in(_rk, 11), (32, 16, 256), jnp.float32)
        _ctx_1024c = jax.random.dirichlet(jax.random.fold_in(_rk, 511), 0.3 * jnp.ones((16,), jnp.float32), (32, 128))
        _ctx_1024t = jnp.einsum('bsk,bkd->bsd', _ctx_1024c, _ctx_1024P)
        _ctx_1024t = _ctx_1024t * jax.lax.rsqrt(jnp.mean(jnp.square(_ctx_1024t)) + 1e-12) * 0.953939
        ctx_1024 = -1.52775e-05 + 0.999936 * (_ctx_1024t + 0.3 * jax.random.normal(jax.random.fold_in(_rk, 611), (32, 128, 256), jnp.float32))
        _g = jax.random.normal(jax.random.fold_in(_rk, 9001), (2, 1), jnp.float32)
        _g = jnp.sign(_g) * jnp.maximum(jnp.abs(_g), 1.0) + (_g == 0) * 1.0
        g_xattn = _g[0]
        g_ffn = _g[1]
        return (x, ctx_1024, g_xattn, g_ffn)
    x, ctx_1024, g_xattn, g_ffn = _rec_inputs()

    def _L0_xattn_setup():
        import jax, jax.numpy as jnp
        import numpy as np
        G = 8
        SCALE = 0.125
        RESID = 1.0
        EPS = 1e-05
        key = jax.random.key(seed)
        ks = jax.random.split(key, 9)
        B, C, D = (64, 128, 256)
        s = 0.02
        return {'inp_q': jax.random.normal(ks[0], (B, C, D), jnp.float32), 'inp_k': jax.random.normal(ks[1], (B, C, D), jnp.float32), 'inp_v': jax.random.normal(ks[2], (B, C, D), jnp.float32), 'Wt': jax.random.normal(ks[3], (C, C), jnp.float32) * s, 'Wp': jax.random.normal(ks[4], (C, C), jnp.float32) * s, 'Wg': jax.random.normal(ks[5], (C, C), jnp.float32) * s, 'Wz': jax.random.normal(ks[6], (G, C // G, C // G), jnp.float32) * s, 'gamma': jax.random.normal(ks[7], (C,), jnp.float32), 'beta': jax.random.normal(ks[8], (C,), jnp.float32)}
    _L0_xattn_all = _L0_xattn_setup()
    _L0_xattn_in = {k: v for k, v in _L0_xattn_all.items() if k in ('Wt', 'Wp', 'Wg', 'Wz', 'gamma', 'beta')}
    del _L0_xattn_all

    def _L0_ffn_setup():
        import jax, jax.numpy as jnp
        import numpy as np
        HID = 256
        INTER = 1024
        RDIM = 128
        HEADS = 4
        NUM_EXPERTS = 4096
        NUM_KEYS = 128
        TOPK = 8
        B, T = (2, 512)
        key = jax.random.key(seed)
        ks = jax.random.split(key, 8)
        s = lambda fan_in: 1.0 / np.sqrt(fan_in)
        return {'hidden_states': jax.random.normal(ks[0], (B, T, HID), jnp.float32), 'Wq': jax.random.normal(ks[1], (HEADS * RDIM, HID), jnp.float32) * s(HID), 'keys': jax.random.normal(ks[2], (HEADS, NUM_KEYS, 2, RDIM // 2), jnp.float32) * s(RDIM // 2), 'down_embed': jax.random.normal(ks[3], (NUM_EXPERTS, HID), jnp.float32) * 0.02, 'up_embed': jax.random.normal(ks[4], (NUM_EXPERTS, HID), jnp.float32) * 0.02, 'Wg': jax.random.normal(ks[5], (INTER, HID), jnp.float32) * s(HID), 'Wu': jax.random.normal(ks[6], (INTER, HID), jnp.float32) * s(HID), 'Wd': jax.random.normal(ks[7], (HID, INTER), jnp.float32) * s(INTER)}
    _L0_ffn_all = _L0_ffn_setup()
    _L0_ffn_in = {k: v for k, v in _L0_ffn_all.items() if k in ('Wq', 'keys', 'down_embed', 'up_embed', 'Wg', 'Wu', 'Wd')}
    del _L0_ffn_all
    return {'x': x, 'ctx_1024': ctx_1024, 'g_xattn': g_xattn, 'g_ffn': g_ffn, 'L0_xattn_Wt': _L0_xattn_in['Wt'], 'L0_xattn_Wp': _L0_xattn_in['Wp'], 'L0_xattn_Wg': _L0_xattn_in['Wg'], 'L0_xattn_Wz': _L0_xattn_in['Wz'], 'L0_xattn_gamma': _L0_xattn_in['gamma'], 'L0_xattn_beta': _L0_xattn_in['beta'], 'L0_ffn_Wq': _L0_ffn_in['Wq'], 'L0_ffn_keys': _L0_ffn_in['keys'], 'L0_ffn_down_embed': _L0_ffn_in['down_embed'], 'L0_ffn_up_embed': _L0_ffn_in['up_embed'], 'L0_ffn_Wg': _L0_ffn_in['Wg'], 'L0_ffn_Wu': _L0_ffn_in['Wu'], 'L0_ffn_Wd': _L0_ffn_in['Wd']}

def reference(x, ctx_1024, g_xattn, g_ffn, L0_xattn_Wt, L0_xattn_Wp, L0_xattn_Wg, L0_xattn_Wz, L0_xattn_gamma, L0_xattn_beta, L0_ffn_Wq, L0_ffn_keys, L0_ffn_down_embed, L0_ffn_up_embed, L0_ffn_Wg, L0_ffn_Wu, L0_ffn_Wd):
    import jax
    import jax.numpy as jnp

    def _L0_xattn_ref(inp_q, inp_k, inp_v, Wt, Wp, Wg, Wz, gamma, beta):
        import jax, jax.numpy as jnp
        import numpy as np
        G = 8
        SCALE = 0.125
        RESID = 1.0
        EPS = 1e-05
        b, C, d = inp_v.shape
        cg = C // G
        t = jnp.einsum('oc,bcd->bod', Wt, inp_v)
        p = jnp.einsum('oc,bcd->bod', Wp, inp_q)
        g = jnp.einsum('oc,bcd->bod', Wg, inp_k)
        tg = t.reshape(b, G, cg, d)
        pg = p.reshape(b, G, cg, d)
        gg = g.reshape(b, G, cg, d)
        att = jnp.einsum('bgcd,bgcd->bg', pg, gg) * SCALE
        x = att[:, :, None, None] * tg
        x = jnp.einsum('goc,bgcd->bgod', Wz, x)
        mean = x.mean(axis=(2, 3), keepdims=True)
        var = x.var(axis=(2, 3), keepdims=True)
        xn = (x - mean) / jnp.sqrt(var + EPS)
        xn = xn.reshape(b, C, d) * gamma[None, :, None] + beta[None, :, None]
        return xn + inp_v * RESID

    def _L0_ffn_ref(hidden_states, Wq, keys, down_embed, up_embed, Wg, Wu, Wd):
        import jax, jax.numpy as jnp
        import numpy as np
        HID = 256
        INTER = 1024
        RDIM = 128
        HEADS = 4
        NUM_EXPERTS = 4096
        NUM_KEYS = 128
        TOPK = 8
        B, T = (2, 512)
        b, t, _ = hidden_states.shape
        q = hidden_states @ Wq.T
        q = q.reshape(b, t, 2, HEADS, RDIM // 2)
        q = jnp.transpose(q, (2, 0, 1, 3, 4))
        sim = jnp.einsum('pbthn,hkpn->pbthk', q, keys)
        sx, ix = jax.lax.top_k(sim[0], TOPK)
        sy, iy = jax.lax.top_k(sim[1], TOPK)
        all_scores = (sx[..., :, None] + sy[..., None, :]).reshape(b, t, HEADS, TOPK * TOPK)
        all_indices = (ix[..., :, None] * NUM_KEYS + iy[..., None, :]).reshape(b, t, HEADS, TOPK * TOPK)
        scores, pk = jax.lax.top_k(all_scores, TOPK)
        indices = jnp.take_along_axis(all_indices, pk, axis=-1)
        down = down_embed[indices]
        up = up_embed[indices]
        w = jnp.einsum('btd,bthkd->bthk', hidden_states, down)
        w = jax.nn.silu(w) * jax.nn.softmax(scores, axis=-1)
        experts_states = jnp.einsum('bthk,bthkd->btd', w, up)
        mlp = jax.nn.silu(hidden_states @ Wg.T) * (hidden_states @ Wu.T) @ Wd.T
        return mlp + experts_states
    x = x + jnp.tanh(g_xattn[0]) * _L0_xattn_ref(_layernorm(x, axis=-1), ctx_1024, ctx_1024, L0_xattn_Wt, L0_xattn_Wp, L0_xattn_Wg, L0_xattn_Wz, L0_xattn_gamma, L0_xattn_beta)
    x = x + jnp.tanh(g_ffn[0]) * _L0_ffn_ref(_layernorm(x, axis=-1), L0_ffn_Wq, L0_ffn_keys, L0_ffn_down_embed, L0_ffn_up_embed, L0_ffn_Wg, L0_ffn_Wu, L0_ffn_Wd)
    return x

_drawn_inputs = setup_inputs


def setup_inputs(seed=0):
    import zlib

    import numpy as np

    out = dict(_drawn_inputs(seed))
    spreads = {}
    factors = {'L0_ffn_Wq': 8.0, 'L0_ffn_keys': 8.0, 'L0_ffn_down_embed': 8.0, 'L0_ffn_up_embed': 8.0}
    for name, (base, spread) in spreads.items():
        noise = np.random.default_rng([zlib.crc32(name.encode()), seed]).standard_normal(out[name].shape)
        drawn = base * np.exp(spread * noise) if base else spread * noise
        out[name] = jnp.asarray(drawn.astype(out[name].dtype))
    for name, factor in factors.items():
        out[name] = (out[name] * factor).astype(out[name].dtype)
    return out
```

```python
from collections import namedtuple
from contextlib import ExitStack

import concourse.bass as bass
from concourse import mybir

F32 = mybir.dt.float32
BF16 = mybir.dt.bfloat16
I32 = mybir.dt.int32
U16 = mybir.dt.uint16
ALU = mybir.AluOpType
ACT = mybir.ActivationFunctionType
AX_X = mybir.AxisListType.X

P = 128
TOPK = 8
EPS = 1e-5
ATT_SCALE = 0.125
RSQRT_MAGIC = float(0x5F3759DF)

Tile = namedtuple("Tile", "t par half")


def tile_at(pair, k):
    return Tile(2 * pair + k, k % 2, pair + k // 2)


def need(eng, sem, value):
    if not (isinstance(value, int) and value <= 0):
        eng.wait_ge(sem, value)


def hold(eng, sem):
    eng.sem_inc(sem, 1)


class Chain:

    def __init__(self, eng, sem, per_tile, held):
        self.eng, self.sem, self.per_tile, self.held = eng, sem, per_tile, held

    def begin(self, t):
        self.base, self.n = t * self.per_tile, 0

    def did(self, instruction):
        instruction.then_inc(self.sem, 1)
        self.n += 1

    def settle(self):
        self.eng.wait_ge(self.sem, self.base + self.n)

    def settle_apart(self):
        self.settle()
        hold(self.eng, self.held)

    def end(self):
        assert self.n == self.per_tile, self.n


def gated_block(nc, x, ctx, attn_w, wz_t, cols, wq, keys_t, table, last_row, wg_t, wu_t, wd_t,
                consts, iota8, out):
    B, _, D = x.shape
    HEADS = keys_t.shape[1] // 2
    NH2 = 2 * HEADS
    KN = wq.shape[0]
    NKEYS = keys_t.shape[2]
    INTER = wg_t.shape[2]
    KT = D // P
    HALF = INTER // 2
    HC = HALF // P
    SLOTS = HEADS * TOPK
    GS = 4
    GROUPS = SLOTS // GS
    LAST = table.shape[0] - 1
    NG = wz_t.shape[0]
    CG = wz_t.shape[1]
    STEPS = 2 * GROUPS
    FRONT = 56

    with ExitStack() as stack:
        def sb(name, shape, dt=F32):
            return stack.enter_context(nc.sbuf_tensor(name, shape, dt))

        def bank(name):
            return stack.enter_context(nc.psum_tensor(name, [P, 512], F32))

        def sem(name):
            return stack.enter_context(nc.semaphore(name))

        attn_sb = sb("attn_sb", [P, 3, P])
        wz_bd = sb("wz_bd", [P, P])
        wzt_sb = sb("wzt_sb", [P, P])
        cols_sb = sb("cols_sb", [P, 4])
        gains = sb("gains", [P, 2])
        gain_gamma = sb("gain_gamma", [P, 1])
        gain_beta = sb("gain_beta", [P, 1])
        gain_ffn = sb("gain_ffn", [P, 1])
        wq_sb = sb("wq_sb", [KN, NH2, D])
        keys_sb = sb("keys_sb", [KN, NH2, NKEYS])
        wk_sb = sb("wk_sb", [P, KT, NH2 * NKEYS])
        last_sb = sb("last_sb", [P, 2 * D])
        wg_sb = sb("wg_sb", [P, KT, INTER])
        wu_sb = sb("wu_sb", [P, KT, INTER])
        wd_sb = sb("wd_sb", [P, INTER // P, D])
        consts_sb = sb("consts_sb", [P, 2, P])
        iota_sb = sb("iota_sb", [P, TOPK], U16)
        ident = consts_sb[:, 0, :]
        group_mean = consts_sb[:, 1, :]
        wp_attn, wg_attn, wt_attn = (attn_sb[:, k, :] for k in range(3))

        x_sb = sb("x_sb", [P, 2, D])
        ctx_sb = sb("ctx_sb", [P, 2, D])
        x1 = sb("x1", [P, 2, D])
        h = sb("h", [P, 2, D])
        h_t = sb("h_t", [P, 2, KT, P])
        idx = sb("idx", [P, 2, SLOTS], I32)
        pv = sb("pv", [P, 2, SLOTS + 1])
        dots = sb("dots", [P, 2, SLOTS + 1])
        th = sb("th", [P, 2, SLOTS + 1])
        thd = sb("thd", [P, 2, SLOTS + 1])
        w = sb("w", [P, 2, SLOTS + 1])
        o_sb = sb("o_sb", [P, 2, D])
        xn = sb("xn", [P, D])
        g_copy = sb("g_copy", [P, D])
        y_sb = sb("y_sb", [P, D])
        att_out = sb("att_out", [P, D])
        products = sb("products", [P, 2 * GS, D])
        bn = sb("bn", [P, 3, 6])
        mv = sb("mv", [P, 2, 2])
        rowstats = sb("rowstats", [P, 3])
        sc = sb("sc", [P, 32])
        top = sb("top", [P, NH2, TOPK])
        top_ix = sb("top_ix", [P, NH2, TOPK], U16)
        pair_sum = sb("pair_sum", [P, HEADS, TOPK, TOPK])
        best = sb("best", [P, HEADS, TOPK])
        best_ix = sb("best_ix", [P, SLOTS], U16)
        rank = sb("rank", [P, NH2 * TOPK], U16)
        onehot = sb("onehot", [P, NH2 * TOPK, TOPK], BF16)
        picked = sb("picked", [P, NH2 * TOPK, TOPK], BF16)
        key_no = sb("key_no", [P, NH2 * TOPK])
        shifted = sb("shifted", [P, HEADS, TOPK])
        expo = sb("expo", [P, HEADS, TOPK])
        exp_sum = sb("exp_sum", [P, HEADS])
        exp_inv = sb("exp_inv", [P, HEADS])
        prob = sb("prob", [P, SLOTS])
        clamped = sb("clamped", [P, SLOTS])
        mlp_th = sb("mlp_th", [P, HALF])
        mlp_g = sb("mlp_g", [P, HALF])
        mlp_m = sb("mlp_m", [P, HALF])
        m_t = sb("m_t", [P, 2, HC, P])
        rows = sb("rows", [P, SLOTS, 2 * D])
        diag = sb("diag", [P, 2, GS + 1, P])

        ps_p = bank("ps_p")
        ps_gz = bank("ps_gz")
        ps_sim = [bank("ps_sim0"), bank("ps_sim1")]
        ps_a = bank("ps_a")
        ps_u = bank("ps_u")
        ps_t = bank("ps_t")
        ps_acc = bank("ps_acc")
        STAT = D

        x_loaded = [sem("x_loaded0"), sem("x_loaded1")]
        attn_loaded = sem("attn_loaded")
        wz_zeroed = sem("wz_zeroed")
        wz_loaded = sem("wz_loaded")
        cols_loaded = sem("cols_loaded")
        keys_loaded = sem("keys_loaded")
        last_loaded = sem("last_loaded")
        mlp_loaded = sem("mlp_loaded")
        consts_loaded = sem("consts_loaded")
        stored = sem("stored")
        gains_ready = sem("gains_ready")
        setup_dve = sem("setup_dve")
        wzt_ps_ready = sem("wzt_ps_ready")
        wzt_ready = sem("wzt_ready")
        wk_ps_ready = sem("wk_ps_ready")
        wk_ready = sem("wk_ready")
        front = sem("front")
        dve_held = sem("dve_held")
        pool_held = sem("pool_held")
        sp_held = sem("sp_held")
        xn_ready = sem("xn_ready")
        gz_ready = sem("gz_ready")
        p_ready = sem("p_ready")
        g_copied = sem("g_copied")
        stats_ready = sem("stats_ready")
        avg_ready = sem("avg_ready")
        q_ready = sem("q_ready")
        xc_used = sem("xc_used")
        affine_ready = sem("affine_ready")
        att_ready = sem("att_ready")
        h_ready = sem("h_ready")
        ht_ps_ready = sem("ht_ps_ready")
        ht_ready = sem("ht_ready")
        sims_ready = sem("sims_ready")
        sims_used = sem("sims_used")
        idx_ready = sem("idx_ready")
        shift_ready = sem("shift_ready")
        exp_ready = sem("exp_ready")
        gathered = [sem(f"gathered{g}") for g in range(GROUPS)]
        dots_ready = sem("dots_ready")
        th_ready = sem("th_ready")
        thd_ready = sem("thd_ready")
        w_ready = sem("w_ready")
        diag_ready = sem("diag_ready")
        rows_cleared = sem("rows_cleared")
        rows_used = sem("rows_used")
        up_ready = sem("up_ready")
        mlp_th_ready = sem("mlp_th_ready")
        mlp_g_ready = sem("mlp_g_ready")
        m_ready = sem("m_ready")
        mt_ps_ready = sem("mt_ps_ready")
        mt_ready = sem("mt_ready")
        out_ready = sem("out_ready")

        block = stack.enter_context(nc.Block())

        def pipeline(tile, loop):
            tile(tile_at(0, 0), first=True)
            with loop(0, B // 2 - 1) as i:
                tile(tile_at(i, 1))
                tile(tile_at(i, 2))
            tile(tile_at(B // 2 - 1, 1), last=True)

        def following(c):
            return Tile(c.t + 1, 1 - c.par, c.half + c.par)

        def preceding(c):
            return Tile(c.t - 1, 1 - c.par, c.half - (1 - c.par))

        @block.sync
        def _(sp):
            def load(c):
                need(sp, xc_used, c.t - 1)
                sp.dma_start(x_sb[:, c.par, :], x[c.t, :, :]).then_inc(x_loaded[c.par], 16)
                sp.dma_start(ctx_sb[:, c.par, :], ctx[c.t, :, :]).then_inc(x_loaded[c.par], 16)

            def store(c):
                sp.wait_ge(out_ready, c.t + 1)
                sp.dma_start(out[c.t, :, :], o_sb[:, c.par, :]).then_inc(stored, 16)
                sp.wait_ge(stored, 16 * (c.t + 1))
                hold(sp, sp_held)

            load(tile_at(0, 0))
            sp.dma_start(attn_sb[:, :, :], attn_w).then_inc(attn_loaded, 16)
            sp.wait_ge(wz_zeroed, 1)
            for g in range(NG):
                sp.dma_start(wz_bd[CG * g:CG * g + CG, CG * g:CG * g + CG], wz_t[g, :, :]).then_inc(wz_loaded, 16)
            sp.dma_start(keys_sb[:, :, :], keys_t).then_inc(keys_loaded, 16)
            sp.dma_start(wq_sb[:, :, :], wq).then_inc(keys_loaded, 16)
            sp.dma_start(last_sb[:, :], last_row).then_inc(last_loaded, 16)

            def tile(c, first=False, last=False):
                if not last:
                    load(following(c))
                if not first:
                    store(preceding(c))

            pipeline(tile, sp.Fori)
            store(tile_at(B // 2 - 1, 1))

        @block.gpsimd
        def _(pool):
            for g in range(GROUPS):
                pool.memset(rows[:, GS * g:GS * (g + 1), :], 0.0).then_inc(rows_cleared, 1)
            pool.wait_ge(rows_cleared, GROUPS)

            def tile(c, first=False, last=False):
                pool.wait_ge(idx_ready, c.t + 1)
                for g in range(GROUPS):
                    need(pool, rows_used, GROUPS * (c.t - 1) + g + 1)
                    hold(pool, pool_held)
                    for s in range(GS * g, GS * (g + 1)):
                        pool.indirect_dma_start(
                            rows[:, s, :], None, table,
                            bass.IndirectOffsetOnAxis(ap=idx[:, c.par, s:s + 1], axis=0),
                            bounds_check=LAST - 1, oob_is_err=False).then_inc(gathered[g], 16)

            pipeline(tile, pool.Fori)

        @block.vector
        def _(dve):
            chain = Chain(dve, front, FRONT, dve_held)

            def rsqrt(v, y, scratch):
                chain.did(dve.tensor_scalar(y.bitcast(I32), v.bitcast(I32), -0.5, RSQRT_MAGIC, ALU.mult, ALU.add))
                for _ in range(2):
                    u, a, b = (scratch[:, k:k + 1] for k in range(3))
                    chain.settle()
                    chain.did(dve.scalar_tensor_tensor(out=u, in0=y, scalar=y, in1=v, op0=ALU.mult, op1=ALU.mult))
                    chain.settle()
                    chain.did(dve.tensor_scalar(a, u, 0.375, -1.25, ALU.mult, ALU.add))
                    chain.settle()
                    chain.did(dve.tensor_scalar(b, a, u, 1.875, ALU.mult, ALU.add))
                    chain.settle()
                    chain.did(dve.tensor_scalar(y, y, b, None, ALU.mult))
                chain.settle()

            def normed(src, k):
                mean, var = mv[:, k, 0:1], sc[:, 8 * k:8 * k + 1]
                rstd = sc[:, 8 * k + 1:8 * k + 2]
                chain.did(dve.bn_stats(bn[:, k, :], src))
                chain.settle_apart()
                chain.did(dve.bn_aggr(mv[:, k, :], bn[:, k, :]))
                chain.settle()
                chain.did(dve.tensor_scalar(var, mv[:, k, 1:2], EPS, None, ALU.add))
                chain.settle()
                rsqrt(var, rstd, sc[:, 8 * k + 2:8 * k + 5])
                return mean, rstd

            mean_c, var_c = rowstats[:, 1:2], rowstats[:, 2:3]
            sum_g, mean_g = sc[:, 16:17], sc[:, 17:18]
            dm, q, att2, var_x, rs_x = (sc[:, k:k + 1] for k in range(18, 23))
            scale_x, shift_x = sc[:, 23:24], sc[:, 24:25]

            def norm_x(n):
                chain.begin(n.t)
                dve.wait_ge(x_loaded[n.par], 32 * (n.half + 1))
                mean, rstd = normed(x_sb[:, n.par, :], 0)
                need(dve, p_ready, n.t)
                dve.tensor_scalar(xn[:, :], x_sb[:, n.par, :], mean, rstd, ALU.subtract, ALU.mult).then_inc(xn_ready, 1)

            def z_stats(n):
                dve.wait_ge(g_copied, n.t + 1)
                chain.did(dve.bn_stats(bn[:, 2, :], ps_gz[:, D:2 * D]))
                dve.scalar_tensor_tensor(out=y_sb[:, :], in0=ctx_sb[:, n.par, :], scalar=gains[:, 0:1],
                                         in1=x_sb[:, n.par, :], op0=ALU.mult, op1=ALU.add).then_inc(xc_used, 1)
                chain.settle_apart()
                dve.bn_aggr(rowstats[:, 1:3], bn[:, 2, :]).then_inc(stats_ready, 1)

            def pg_sums(n):
                dve.wait_ge(p_ready, n.t + 1)
                dve.tensor_tensor_reduce(g_copy[:, :], ps_p[:, 0:D], g_copy[:, :], 1.0, 0.0, ALU.mult, ALU.add,
                                         rowstats[:, 0:1]).then_inc(stats_ready, 1)

            def spread(n):
                dve.wait_ge(avg_ready, 2 * n.t + 1)
                chain.did(dve.tensor_copy(sc[:, 16:18], ps_p[:, STAT:STAT + 2]))
                chain.settle()
                chain.did(dve.tensor_scalar(dm, mean_c, mean_g, None, ALU.subtract))
                chain.settle()
                dve.scalar_tensor_tensor(out=q, in0=dm, scalar=dm, in1=var_c, op0=ALU.mult,
                                         op1=ALU.add).then_inc(q_ready, 1)
                k = (ATT_SCALE * CG) ** 2
                chain.did(dve.tensor_scalar(att2, sum_g, sum_g, k, ALU.mult, ALU.mult))

            def affine(n):
                dve.wait_ge(avg_ready, 2 * n.t + 2)
                chain.settle()
                chain.did(dve.tensor_scalar(var_x, ps_p[:, STAT + 2:STAT + 3], att2, EPS, ALU.mult, ALU.add))
                chain.settle()
                rsqrt(var_x, rs_x, sc[:, 25:28])
                dve.tensor_scalar(scale_x, rs_x, sum_g, gain_gamma[:, :], ALU.mult, ALU.mult).then_inc(affine_ready, 1)
                dve.wait_ge(affine_ready, n.t + 1)
                chain.did(dve.scalar_tensor_tensor(out=shift_x, in0=scale_x, scalar=mean_g, in1=gain_beta[:, :],
                                                   op0=ALU.mult, op1=ALU.subtract))

            def residual(n):
                dve.wait_ge(att_ready, n.t + 1)
                dve.wait_ge(xc_used, n.t + 1)
                chain.settle()
                chain.did(dve.scalar_tensor_tensor(out=x1[:, n.par, :], in0=y_sb[:, :], scalar=shift_x,
                                                   in1=att_out[:, :], op0=ALU.subtract, op1=ALU.add))
                chain.settle()
                mean, rstd = normed(x1[:, n.par, :], 1)
                dve.tensor_scalar(h[:, n.par, :], x1[:, n.par, :], mean, rstd, ALU.subtract,
                                  ALU.mult).then_inc(h_ready, 1)
                dve.wait_ge(h_ready, n.t + 1)
                chain.did(dve.tensor_tensor_reduce(y_sb[:, :], h[:, n.par, :], last_sb[:, 0:D], 1.0, 0.0, ALU.mult,
                                                   ALU.add, dots[:, n.par, 0:1]))

            def key_tops(n):
                def sim(ph):
                    return ps_sim[ph // HEADS][:, NKEYS * (ph % HEADS):NKEYS * (ph % HEADS + 1)]

                dve.wait_ge(sims_ready, n.t + 1)
                hold(dve, dve_held)
                for ph in range(NH2):
                    last = dve.max(top[:, ph, :], sim(ph))
                chain.did(last)
                chain.settle_apart()
                for ph in range(NH2):
                    last = dve.max_index(top_ix[:, ph, :], top[:, ph, :], sim(ph))
                last.then_inc(sims_used, 1)

            def pair_tops(n):
                chain.did(dve.tensor_tensor(
                    pair_sum[:, :, :, :],
                    top[:, 0:HEADS, :].unsqueeze(3).broadcast_to([P, HEADS, TOPK, TOPK]),
                    top[:, HEADS:NH2, :].unsqueeze(2).broadcast_to([P, HEADS, TOPK, TOPK]), ALU.add))
                chain.settle_apart()
                sums = pair_sum[:, :, :, :].rearrange("p h a b -> p h (a b)")
                for hd in range(HEADS):
                    last = dve.max(best[:, hd, :], sums[:, hd, :])
                chain.did(last)
                chain.settle_apart()
                for hd in range(HEADS):
                    last = dve.max_index(best_ix[:, TOPK * hd:TOPK * (hd + 1)], best[:, hd, :], sums[:, hd, :])
                chain.did(last)
                dve.tensor_tensor(shifted[:, :, :], best[:, :, :],
                                  best[:, :, 0:1].broadcast_to([P, HEADS, TOPK]),
                                  ALU.subtract).then_inc(shift_ready, 1)

            def decode(n):
                chain.settle()
                chain.did(dve.tensor_scalar(rank[:, 0:SLOTS], best_ix[:, :], 3, None, ALU.logical_shift_right))
                chain.did(dve.tensor_scalar(rank[:, SLOTS:2 * SLOTS], best_ix[:, :], TOPK - 1, None, ALU.bitwise_and))
                chain.settle()
                chain.did(dve.tensor_tensor(onehot[:, :, :],
                                            rank[:, :].unsqueeze(2).broadcast_to([P, NH2 * TOPK, TOPK]),
                                            iota_sb[:, :].unsqueeze(1).broadcast_to([P, NH2 * TOPK, TOPK]),
                                            ALU.is_equal))
                chain.settle()
                dve.wait_ge(sims_used, n.t + 1)
                chain.did(dve.tensor_tensor(picked[:, :, :].rearrange("p (f k) a -> p f k a", k=TOPK),
                                            onehot[:, :, :].rearrange("p (f k) a -> p f k a", k=TOPK),
                                            top_ix[:, :, :].unsqueeze(2).broadcast_to([P, NH2, TOPK, TOPK]),
                                            ALU.mult))
                chain.settle()
                chain.did(dve.tensor_reduce(key_no[:, :], picked[:, :, :], AX_X, ALU.add))
                chain.settle()
                dve.scalar_tensor_tensor(out=idx[:, n.par, :], in0=key_no[:, 0:SLOTS], scalar=float(NKEYS),
                                         in1=key_no[:, SLOTS:2 * SLOTS], op0=ALU.mult,
                                         op1=ALU.add).then_inc(idx_ready, 1)

            def weights(n):
                dve.wait_ge(exp_ready, n.t + 1)
                chain.did(dve.tensor_reduce(exp_sum[:, :], expo[:, :, :], AX_X, ALU.add))
                chain.settle()
                chain.did(dve.reciprocal(exp_inv[:, :], exp_sum[:, :]))
                chain.settle()
                chain.did(dve.tensor_tensor(prob[:, :].rearrange("p (a k) -> p a k", k=TOPK), expo[:, :, :],
                                            exp_inv[:, :].unsqueeze(2).broadcast_to([P, HEADS, TOPK]), ALU.mult))
                chain.settle()
                dve.wait_ge(idx_ready, n.t + 1)
                chain.did(dve.scalar_tensor_tensor(out=clamped[:, :], in0=idx[:, n.par, :], scalar=float(LAST),
                                                   in1=prob[:, :], op0=ALU.is_ge, op1=ALU.mult))
                chain.did(dve.scalar_tensor_tensor(out=pv[:, n.par, 1:SLOTS + 1], in0=idx[:, n.par, :],
                                                   scalar=float(LAST), in1=prob[:, :], op0=ALU.is_lt, op1=ALU.mult))
                chain.settle()
                chain.did(dve.tensor_reduce(pv[:, n.par, 0:1], clamped[:, :], AX_X, ALU.add))
                chain.settle()
                chain.end()

            def dot(c, s):
                g = s // GS
                if s % GS == 0:
                    dve.wait_ge(gathered[g], 16 * GS * (c.t + 1))
                made = dve.tensor_tensor_reduce(products[:, s % (2 * GS), :], h[:, c.par, :], rows[:, s, 0:D], 1.0, 0.0, ALU.mult,
                                                ALU.add, dots[:, c.par, 1 + s:2 + s])
                if s % GS == GS - 1:
                    made.then_inc(dots_ready, 1)

            def weigh(c, g):
                a, b = (0 if g == 0 else 1 + GS * g), 1 + GS * (g + 1)
                n = GROUPS * c.t + g + 1
                dve.wait_ge(th_ready, n)
                dve.scalar_tensor_tensor(out=thd[:, c.par, a:b], in0=th[:, c.par, a:b], scalar=1.0,
                                         in1=dots[:, c.par, a:b], op0=ALU.add, op1=ALU.mult).then_inc(thd_ready, 1)
                dve.wait_ge(thd_ready, n)
                dve.tensor_tensor(w[:, c.par, a:b], thd[:, c.par, a:b], pv[:, c.par, a:b],
                                  ALU.mult).then_inc(w_ready, 1)

            def mlp_gate(c, hf):
                n = 2 * c.t + hf + 1
                dve.wait_ge(mlp_th_ready, n)
                dve.scalar_tensor_tensor(out=mlp_g[:, :], in0=mlp_th[:, :], scalar=1.0, in1=ps_a[:, :],
                                         op0=ALU.add, op1=ALU.mult).then_inc(mlp_g_ready, 1)
                dve.wait_ge(mlp_g_ready, n)
                need(dve, mt_ps_ready, n - 1)
                dve.tensor_tensor(mlp_m[:, :], mlp_g[:, :], ps_u[:, :], ALU.mult).then_inc(m_ready, 1)

            def finish(c, last=False):
                dve.wait_ge(rows_used, GROUPS * (c.t + 1))
                if last:
                    dve.wait_ge(stored, 16 * (c.t - 1))
                dve.scalar_tensor_tensor(out=o_sb[:, c.par, :], in0=ps_acc[:, 0:D],
                                         scalar=gain_ffn[:, :], in1=x1[:, c.par, :], op0=ALU.mult,
                                         op1=ALU.add).then_inc(out_ready, 1)

            dve.memset(wz_bd[:, :], 0.0).then_inc(wz_zeroed, 1)
            first = tile_at(0, 0)
            norm_x(first)
            dve.wait_ge(wzt_ps_ready, 1)
            dve.tensor_copy(wzt_sb[:, :], ps_acc[:, 0:P]).then_inc(wzt_ready, 1)
            dve.wait_ge(gains_ready, 1)
            dve.wait_ge(cols_loaded, 16)
            dve.tensor_scalar(gain_gamma[:, :], cols_sb[:, 0:1], gains[:, 0:1], ATT_SCALE * CG, ALU.mult,
                              ALU.mult).then_inc(setup_dve, 1)
            dve.tensor_scalar(gain_beta[:, :], cols_sb[:, 1:2], gains[:, 0:1], None, ALU.mult).then_inc(setup_dve, 1)
            dve.tensor_scalar(gain_ffn[:, :], gains[:, 1:2], 0.5, None, ALU.mult).then_inc(setup_dve, 1)
            dve.wait_ge(setup_dve, 3)
            z_stats(first)
            pg_sums(first)
            spread(first)
            affine(first)
            dve.wait_ge(last_loaded, 16)
            residual(first)
            key_tops(first)
            pair_tops(first)
            dve.wait_ge(consts_loaded, 32)
            decode(first)
            weights(first)

            def tile(c, first=False, last=False):
                n, b = following(c), preceding(c)
                for k in range(STEPS):
                    if k == 0:
                        if not first:
                            weigh(b, GROUPS - 1)
                        if not last:
                            norm_x(n)
                    if k == 1 and not last:
                        z_stats(n)
                    if k == 2 and not last:
                        pg_sums(n)
                    if k == 3 and not last:
                        spread(n)
                    if k == 4 and not last:
                        affine(n)
                    if k == 3 and not first:
                        finish(b)
                    if k == 6 and not last:
                        residual(n)
                    if k == 10 and not last:
                        key_tops(n)
                    if k == 11 and not last:
                        pair_tops(n)
                    if k == 12 and not last:
                        decode(n)
                    if k == 13 and not last:
                        weights(n)
                    for s in range(k * GS // 2, (k + 1) * GS // 2):
                        dot(c, s)
                    if k >= 2 and k % 2 == 0:
                        weigh(c, k // 2 - 1)
                    if k == 5:
                        mlp_gate(c, 0)
                    if k == 13:
                        mlp_gate(c, 1)

            pipeline(tile, dve.Fori)
            end = tile_at(B // 2 - 1, 1)
            weigh(end, GROUPS - 1)
            finish(end, last=True)

        @block.scalar
        def _(act):
            act.dma_start(cols_sb[:, :], cols).then_inc(cols_loaded, 16)
            act.dma_start(consts_sb[:, :, :], consts).then_inc(consts_loaded, 16)
            act.dma_start(iota_sb[:, :], iota8).then_inc(consts_loaded, 16)
            act.dma_start(wg_sb[:, :, :], wg_t).then_inc(mlp_loaded, 16)
            act.dma_start(wu_sb[:, :, :], wu_t).then_inc(mlp_loaded, 16)
            act.dma_start(wd_sb[:, :, :], wd_t).then_inc(mlp_loaded, 16)

            def copy_g(n):
                act.wait_ge(gz_ready, n.t + 1)
                need(act, stats_ready, 2 * n.t)
                act.activation(g_copy[:, :], ps_gz[:, 0:D], ACT.Copy).then_inc(g_copied, 1)

            def scale_z(n):
                act.wait_ge(affine_ready, n.t + 1)
                act.activation(att_out[:, :], ps_gz[:, D:2 * D], ACT.Copy, scale=sc[:, 23:24]).then_inc(att_ready, 1)

            def copy_ht(n):
                act.wait_ge(ht_ps_ready, n.t + 1)
                act.activation(h_t[:, n.par, :, :].rearrange("p k t -> p (k t)"), ps_p[:, 0:D],
                               ACT.Copy).then_inc(ht_ready, 1)

            def exps(n):
                act.wait_ge(shift_ready, n.t + 1)
                act.activation(expo[:, :, :], shifted[:, :, :], ACT.Exp).then_inc(exp_ready, 1)

            def tanh_dots(c, g):
                a, b = (0 if g == 0 else 1 + GS * g), 1 + GS * (g + 1)
                act.wait_ge(dots_ready, GROUPS * c.t + g + 1)
                act.activation(th[:, c.par, a:b], dots[:, c.par, a:b], ACT.Tanh, scale=0.5).then_inc(th_ready, 1)

            def diags(c, g):
                act.wait_ge(w_ready, GROUPS * c.t + g + 1)
                need(act, rows_used, GROUPS * c.t + g - 1)
                for j in range(0 if g == 0 else 1, GS + 1):
                    made = act.activation(diag[:, g % 2, j, :], ident, ACT.Copy,
                                          scale=w[:, c.par, GS * g + j:GS * g + j + 1])
                made.then_inc(diag_ready, 1)

            def mlp_tanh(c, hf):
                n = 2 * c.t + hf + 1
                act.wait_ge(up_ready, n)
                need(act, mlp_g_ready, n - 1)
                act.activation(mlp_th[:, :], ps_a[:, :], ACT.Tanh, scale=0.5).then_inc(mlp_th_ready, 1)

            def copy_mt(c, hf):
                act.wait_ge(mt_ps_ready, 2 * c.t + hf + 1)
                act.activation(m_t[:, hf, :, :].rearrange("p k t -> p (k t)"), ps_t[:, :],
                               ACT.Copy).then_inc(mt_ready, 1)

            first = tile_at(0, 0)
            act.wait_ge(cols_loaded, 16)
            act.activation(gains[:, :], cols_sb[:, 2:4], ACT.Tanh).then_inc(gains_ready, 1)
            copy_g(first)
            act.wait_ge(wk_ps_ready, 1)
            wk_flat = wk_sb[:, :, :].rearrange("p k n -> p (k n)")
            for q, src in enumerate((ps_sim[0], ps_sim[1], ps_a, ps_u)):
                act.activation(wk_flat[:, 512 * q:512 * (q + 1)], src[:, :], ACT.Copy).then_inc(wk_ready, 1)
            scale_z(first)
            copy_ht(first)
            exps(first)
            act.wait_ge(consts_loaded, 32)

            def tile(c, first=False, last=False):
                n, b = following(c), preceding(c)
                for k in range(STEPS):
                    if k == 1 and not last:
                        copy_g(n)
                    if k == 1 and not first:
                        diags(b, GROUPS - 1)
                    if k >= 3 and k % 2 == 1:
                        diags(c, k // 2 - 1)
                    if k == 4:
                        mlp_tanh(c, 0)
                    if k == 5 and not last:
                        scale_z(n)
                    if k == 8 and not last:
                        copy_ht(n)
                    if k == 8:
                        copy_mt(c, 0)
                    if k == 12:
                        mlp_tanh(c, 1)
                    if k == 12 and not last:
                        exps(n)
                    if k == 14:
                        copy_mt(c, 1)
                    if k % 2 == 1:
                        tanh_dots(c, k // 2)

            pipeline(tile, act.Fori)
            diags(tile_at(B // 2 - 1, 1), GROUPS - 1)

        @block.tensor
        def _(pe):
            def attn_gz(n):
                pe.wait_ge(x_loaded[n.par], 32 * (n.half + 1))
                need(pe, att_ready, n.t)
                pe.matmul(ps_gz[:, 0:D], wg_attn, ctx_sb[:, n.par, :], start=True, stop=True)
                pe.matmul(ps_gz[:, D:2 * D], wzt_sb[:, :], ctx_sb[:, n.par, :], start=True,
                          stop=True).then_inc(gz_ready, 1)

            def attn_p(n):
                pe.wait_ge(xn_ready, n.t + 1)
                need(pe, ht_ready, n.t)
                pe.matmul(ps_p[:, 0:D], wp_attn, xn[:, :], start=True, stop=True).then_inc(p_ready, 1)

            def group_means(n):
                pe.wait_ge(stats_ready, 2 * n.t + 2)
                pe.matmul(ps_p[:, STAT:STAT + 2], group_mean, rowstats[:, 0:2], start=True,
                          stop=True).then_inc(avg_ready, 1)

            def group_var(n):
                pe.wait_ge(q_ready, n.t + 1)
                pe.matmul(ps_p[:, STAT + 2:STAT + 3], group_mean, sc[:, 19:20], start=True,
                          stop=True).then_inc(avg_ready, 1)

            def turn_h(n):
                pe.wait_ge(h_ready, n.t + 1)
                for kt in range(KT):
                    last = pe.transpose(ps_p[:, P * kt:P * (kt + 1)], h[:, n.par, P * kt:P * (kt + 1)], ident)
                last.then_inc(ht_ps_ready, 1)

            def sims(n):
                pe.wait_ge(ht_ready, n.t + 1)
                need(pe, sims_used, n.t)
                for f in range(2):
                    for kt in range(KT):
                        last = pe.matmul(ps_sim[f][:, :], h_t[:, n.par, kt, :], wk_sb[:, kt, 512 * f:512 * (f + 1)],
                                         start=(kt == 0), stop=(kt == KT - 1))
                last.then_inc(sims_ready, 1)

            def mlp_up(c, hf):
                need(pe, m_ready, 2 * c.t + hf)
                for bank_, w_ in ((ps_a, wg_sb), (ps_u, wu_sb)):
                    for kt in range(KT):
                        last = pe.matmul(bank_[:, :], h_t[:, c.par, kt, :], w_[:, kt, HALF * hf:HALF * (hf + 1)],
                                         start=(kt == 0), stop=(kt == KT - 1))
                last.then_inc(up_ready, 1)

            def mlp_turn(c, hf):
                pe.wait_ge(m_ready, 2 * c.t + hf + 1)
                need(pe, mt_ready, 2 * c.t + hf)
                for q in range(HC):
                    turned = pe.transpose(ps_t[:, P * q:P * (q + 1)], mlp_m[:, P * q:P * (q + 1)], ident)
                turned.then_inc(mt_ps_ready, 1)

            def mlp_down(c, hf):
                pe.wait_ge(mt_ready, 2 * c.t + hf + 1)
                for q in range(HC):
                    pe.matmul(ps_acc[:, 0:D], m_t[:, hf, q, :], wd_sb[:, HC * hf + q, :],
                              start=False, stop=False)

            def experts(c, g):
                pe.wait_ge(diag_ready, GROUPS * c.t + g + 1)
                if g == 0:
                    need(pe, out_ready, c.t)
                for j in range(0 if g == 0 else 1, GS + 1):
                    s = GS * g + j
                    up = last_sb[:, D:2 * D] if s == 0 else rows[:, s - 1, D:2 * D]
                    last = pe.matmul(ps_acc[:, 0:D], diag[:, g % 2, j, :], up,
                                     start=(s == 0), stop=(s == SLOTS))
                last.then_inc(rows_used, 1)

            pe.wait_ge(attn_loaded, 16)
            pe.wait_ge(wz_loaded, 16 * NG)
            pe.matmul(ps_acc[:, 0:P], wt_attn, wz_bd[:, :], start=True, stop=True).then_inc(wzt_ps_ready, 1)
            first = tile_at(0, 0)
            attn_p(first)
            pe.wait_ge(wzt_ready, 1)
            attn_gz(first)
            pe.wait_ge(keys_loaded, 32)
            wk_banks = (ps_sim[0], ps_sim[1], ps_a, ps_u)
            for kt in range(KT):
                for ph in range(NH2):
                    at = NH2 * kt + ph
                    last = pe.matmul(wk_banks[at // 4][:, NKEYS * (at % 4):NKEYS * (at % 4 + 1)],
                                     wq_sb[:, ph, P * kt:P * (kt + 1)], keys_sb[:, ph, :], start=True, stop=True)
            last.then_inc(wk_ps_ready, 1)
            pe.wait_ge(consts_loaded, 32)
            group_means(first)
            group_var(first)
            turn_h(first)
            pe.wait_ge(wk_ready, 4)
            sims(first)
            pe.wait_ge(mlp_loaded, 48)

            def tile(c, first=False, last=False):
                n, b = following(c), preceding(c)
                for k in range(STEPS):
                    if k == 0 and not last:
                        attn_gz(n)
                    if k == 0 and not first:
                        experts(b, GROUPS - 2)
                    if k == 1 and not last:
                        attn_p(n)
                    if k == 2 and not first:
                        experts(b, GROUPS - 1)
                    if k == 2:
                        mlp_up(c, 0)
                    if k == 3 and not last:
                        group_means(n)
                    if k == 4 and not last:
                        group_var(n)
                    if k >= 4 and k % 2 == 0:
                        experts(c, k // 2 - 2)
                    if k == 7 and not last:
                        turn_h(n)
                    if k == 7:
                        mlp_turn(c, 0)
                    if k == 8 and not last:
                        sims(n)
                    if k == 9:
                        mlp_down(c, 0)
                    if k == 10:
                        mlp_up(c, 1)
                    if k == 14:
                        mlp_turn(c, 1)
                    if k == 15:
                        mlp_down(c, 1)

            pipeline(tile, pe.Fori)
            for g in (GROUPS - 2, GROUPS - 1):
                experts(tile_at(B // 2 - 1, 1), g)


def kernel(**inputs):
    import numpy as np
    import concourse.bacc as bacc
    from concourse import mybir as _mybir
    from concourse.bass_utils import run_bass_kernel_spmd

    a = {k: np.asarray(v) for k, v in inputs.items()}
    x = a["x"]
    b, c, d = x.shape
    heads, nkeys, _, kn = a["L0_ffn_keys"].shape
    inter = a["L0_ffn_Wg"].shape[0]
    kt = d // c
    cg = a["L0_xattn_Wz"].shape[1]
    table = np.concatenate([a["L0_ffn_down_embed"], a["L0_ffn_up_embed"]], axis=1)
    consts = np.zeros((c, 2, c), np.float32)
    consts[:, 0, :] = np.eye(c, dtype=np.float32)
    consts[:, 1, :] = np.kron(np.eye(c // cg, dtype=np.float32), np.full((cg, cg), 1.0 / cg, np.float32))
    laid = [
        ("x", x),
        ("ctx", a["ctx_1024"]),
        ("attn_w", np.stack([a["L0_xattn_Wp"].T, a["L0_xattn_Wg"].T, a["L0_xattn_Wt"]], axis=1)),
        ("wz_t", a["L0_xattn_Wz"].transpose(0, 2, 1)),
        ("cols", np.stack([a["L0_xattn_gamma"], a["L0_xattn_beta"],
                           np.broadcast_to(a["g_xattn"], (c,)), np.broadcast_to(a["g_ffn"], (c,))], axis=1)),
        ("wq", a["L0_ffn_Wq"].reshape(2 * heads, kn, d).transpose(1, 0, 2)),
        ("keys_t", a["L0_ffn_keys"].transpose(3, 2, 0, 1).reshape(kn, 2 * heads, nkeys)),
        ("table", table),
        ("last_row", np.broadcast_to(table[-1], (c, 2 * d))),
        ("wg_t", a["L0_ffn_Wg"].T.reshape(kt, c, inter).transpose(1, 0, 2)),
        ("wu_t", a["L0_ffn_Wu"].T.reshape(kt, c, inter).transpose(1, 0, 2)),
        ("wd_t", a["L0_ffn_Wd"].T.reshape(inter // c, c, d).transpose(1, 0, 2)),
        ("consts", consts),
        ("iota8", np.tile(np.arange(8, dtype=np.uint16), (c, 1))),
    ]
    nc = bacc.Bacc("TRN2", target_bir_lowering=False, num_devices=1)
    arrays, args = {}, []
    for name, value in laid:
        value = np.ascontiguousarray(value)
        arrays[f"in_{name}"] = value
        args.append(nc.dram_tensor(f"in_{name}", value.shape, _mybir.dt.from_np(value.dtype), kind="ExternalInput").ap())
    args.append(nc.dram_tensor("out_y", x.shape, _mybir.dt.float32, kind="ExternalOutput").ap())
    gated_block(nc, *args)
    return run_bass_kernel_spmd(nc, [arrays], core_ids=[0]).results[0]["out_y"]
```

```python
from collections import namedtuple
from contextlib import ExitStack

import concourse.bass as bass
from concourse import mybir

F32 = mybir.dt.float32
BF16 = mybir.dt.bfloat16
I32 = mybir.dt.int32
U16 = mybir.dt.uint16
ALU = mybir.AluOpType
ACT = mybir.ActivationFunctionType
AX_X = mybir.AxisListType.X

P = 128
TOPK = 8
EPS = 1e-5
ATT_SCALE = 0.125
MINUS_GUESS = float(0x5F3759DF - (1 << 22) - (1 << 31))

Tile = namedtuple("Tile", "t par half")


def tile_at(pair, k):
    return Tile(2 * pair + k, k % 2, pair + k // 2)


def need(eng, sem, value):
    if not (isinstance(value, int) and value <= 0):
        eng.wait_ge(sem, value)


def hold(eng, sem):
    eng.sem_inc(sem, 1)


class Chain:

    def __init__(self, eng, sem, per_tile, held):
        self.eng, self.sem, self.per_tile, self.held = eng, sem, per_tile, held

    def begin(self, t):
        self.base, self.n = t * self.per_tile, 0

    def did(self, instruction):
        instruction.then_inc(self.sem, 1)
        self.n += 1

    def settle(self):
        self.eng.wait_ge(self.sem, self.base + self.n)

    def settle_apart(self):
        self.settle()
        hold(self.eng, self.held)

    def end(self):
        assert self.n == self.per_tile, self.n


def gated_block(nc, x, ctx, attn_w, wz_t, cols, wq, keys_t, table, last_row, wg_t, wu_t, wd_t,
                consts, iota8, out):
    B, _, D = x.shape
    HEADS = keys_t.shape[1] // 2
    NH2 = 2 * HEADS
    KN = wq.shape[0]
    NKEYS = keys_t.shape[2]
    INTER = wg_t.shape[2]
    KT = D // P
    HALF = INTER // 2
    HC = HALF // P
    SLOTS = HEADS * TOPK
    GS = 4
    GROUPS = SLOTS // GS
    LAST = table.shape[0] - 1
    NG = wz_t.shape[0]
    CG = wz_t.shape[1]
    DIAGS = 4
    ATTN_STEPS, FFN_STEPS = 23, 27

    with ExitStack() as stack:
        def sb(name, shape, dt=F32):
            return stack.enter_context(nc.sbuf_tensor(name, shape, dt))

        def bank(name):
            return stack.enter_context(nc.psum_tensor(name, [P, 512], F32))

        def sem(name):
            return stack.enter_context(nc.semaphore(name))

        attn_sb = sb("attn_sb", [P, 3, P])
        wz_bd = sb("wz_bd", [P, P])
        wzt_sb = sb("wzt_sb", [P, P])
        cols_sb = sb("cols_sb", [P, 4])
        gains = sb("gains", [P, 2])
        gain_gamma = sb("gain_gamma", [P, 1])
        gain_beta = sb("gain_beta", [P, 1])
        wq_sb = sb("wq_sb", [KN, NH2, D])
        keys_sb = sb("keys_sb", [KN, NH2, NKEYS])
        wk_sb = sb("wk_sb", [P, KT, NH2 * NKEYS])
        last_sb = sb("last_sb", [P, 2 * D])
        wg_sb = sb("wg_sb", [P, KT, INTER])
        wu_sb = sb("wu_sb", [P, KT, INTER])
        wd_sb = sb("wd_sb", [P, INTER // P, D])
        consts_sb = sb("consts_sb", [P, 2, P])
        iota_sb = sb("iota_sb", [P, TOPK], U16)
        ident = consts_sb[:, 0, :]
        group_mean = consts_sb[:, 1, :]
        wp_attn, wg_attn, wt_attn = (attn_sb[:, k, :] for k in range(3))

        x_sb = sb("x_sb", [P, 2, D])
        ctx_sb = sb("ctx_sb", [P, 2, D])
        x1 = sb("x1", [P, 2, D])
        h = sb("h", [P, 2, D])
        h_t = sb("h_t", [P, 2, KT, P])
        idx = sb("idx", [P, 2, SLOTS], I32)
        pv = sb("pv", [P, 2, SLOTS + 1])
        dots = sb("dots", [P, 2, SLOTS + 1])
        silu = sb("silu", [P, 2, SLOTS + 1])
        w = sb("w", [P, 2, SLOTS + 1])
        o_sb = sb("o_sb", [P, 2, D])
        xn = sb("xn", [P, D])
        g_copy = sb("g_copy", [P, D])
        y_sb = sb("y_sb", [P, D])
        att_out = sb("att_out", [P, D])
        products = sb("products", [P, 2 * GS, D])
        bn = sb("bn", [P, 3, 6])
        mv = sb("mv", [P, 2, 2])
        rowstats = sb("rowstats", [P, 3])
        sc = sb("sc", [P, 32])
        top = sb("top", [P, NH2, TOPK])
        top_ix = sb("top_ix", [P, NH2, TOPK], U16)
        pair_sum = sb("pair_sum", [P, HEADS, TOPK, TOPK])
        best = sb("best", [P, HEADS, TOPK])
        best_ix = sb("best_ix", [P, SLOTS], U16)
        rank = sb("rank", [P, NH2 * TOPK], U16)
        onehot = sb("onehot", [P, NH2 * TOPK, TOPK], BF16)
        picked = sb("picked", [P, NH2 * TOPK, TOPK], BF16)
        key_no = sb("key_no", [P, NH2 * TOPK])
        shifted = sb("shifted", [P, HEADS, TOPK])
        expo = sb("expo", [P, HEADS, TOPK])
        exp_sum = sb("exp_sum", [P, HEADS])
        exp_inv = sb("exp_inv", [P, HEADS])
        prob = sb("prob", [P, SLOTS])
        clamped = sb("clamped", [P, SLOTS])
        mlp_silu = sb("mlp_silu", [P, HALF])
        mlp_m = sb("mlp_m", [P, HALF])
        m_t = sb("m_t", [P, 2, HC, P])
        rows = sb("rows", [P, SLOTS, 2 * D])
        diag = sb("diag", [P, DIAGS, GS + 1, P])

        ps_p = bank("ps_p")
        ps_gz = bank("ps_gz")
        ps_sim = [bank("ps_sim0"), bank("ps_sim1")]
        ps_a = bank("ps_a")
        ps_u = bank("ps_u")
        ps_t = ps_a
        ps_acc = [bank("ps_acc0"), bank("ps_acc1")]
        STAT = D

        x_loaded = [sem("x_loaded0"), sem("x_loaded1")]
        attn_loaded = sem("attn_loaded")
        wz_zeroed = sem("wz_zeroed")
        wz_loaded = sem("wz_loaded")
        cols_loaded = sem("cols_loaded")
        keys_loaded = sem("keys_loaded")
        last_loaded = sem("last_loaded")
        mlp_loaded = sem("mlp_loaded")
        consts_loaded = sem("consts_loaded")
        stored = sem("stored")
        gains_ready = sem("gains_ready")
        setup_dve = sem("setup_dve")
        wzt_ps_ready = sem("wzt_ps_ready")
        wzt_ready = sem("wzt_ready")
        wk_ps_ready = sem("wk_ps_ready")
        wk_ready = sem("wk_ready")
        attn_steps = sem("attn_steps")
        ffn_steps = sem("ffn_steps")
        dve_held = sem("dve_held")
        pool_held = sem("pool_held")
        sp_held = sem("sp_held")
        xn_ready = sem("xn_ready")
        gz_ready = sem("gz_ready")
        p_ready = sem("p_ready")
        g_copied = sem("g_copied")
        stats_ready = sem("stats_ready")
        avg_ready = sem("avg_ready")
        q_ready = sem("q_ready")
        xc_used = sem("xc_used")
        affine_ready = sem("affine_ready")
        att_ready = sem("att_ready")
        h_ready = sem("h_ready")
        ht_ps_ready = sem("ht_ps_ready")
        ht_ready = sem("ht_ready")
        sims_ready = sem("sims_ready")
        sims_used = sem("sims_used")
        idx_ready = sem("idx_ready")
        shift_ready = sem("shift_ready")
        exp_ready = sem("exp_ready")
        gathered = [sem(f"gathered{g}") for g in range(GROUPS)]
        dots_ready = sem("dots_ready")
        silu_ready = sem("silu_ready")
        w_ready = sem("w_ready")
        diag_ready = sem("diag_ready")
        rows_cleared = sem("rows_cleared")
        rows_used = sem("rows_used")
        up_ready = sem("up_ready")
        mlp_silu_ready = sem("mlp_silu_ready")
        m_ready = sem("m_ready")
        mt_ps_ready = sem("mt_ps_ready")
        mt_ready = sem("mt_ready")
        x1_copied = sem("x1_copied")
        out_ready = sem("out_ready")

        block = stack.enter_context(nc.Block())

        def pipeline(tile, loop):
            tile(tile_at(0, 0), False, True, True)
            tile(tile_at(0, 1), True, True, True)
            with loop(1, B // 2 - 1) as i:
                tile(tile_at(i, 0), True, True, True)
                tile(tile_at(i, 1), True, True, True)
            tile(tile_at(B // 2 - 1, 0), True, True, False)
            tile(tile_at(B // 2 - 1, 1), True, False, False)

        def following(c):
            return Tile(c.t + 1, 1 - c.par, c.half + c.par)

        def second_after(c):
            return Tile(c.t + 2, c.par, c.half + 1)

        def preceding(c):
            return Tile(c.t - 1, 1 - c.par, c.half - (1 - c.par))

        @block.sync
        def _(sp):
            def load(c):
                need(sp, xc_used, c.t - 1)
                sp.dma_start(x_sb[:, c.par, :], x[c.t, :, :]).then_inc(x_loaded[c.par], 16)
                sp.dma_start(ctx_sb[:, c.par, :], ctx[c.t, :, :]).then_inc(x_loaded[c.par], 16)

            def store(c):
                sp.wait_ge(out_ready, c.t + 1)
                sp.dma_start(out[c.t, :, :], o_sb[:, c.par, :]).then_inc(stored, 16)
                sp.wait_ge(stored, 16 * (c.t + 1))
                hold(sp, sp_held)

            load(tile_at(0, 0))
            sp.dma_start(attn_sb[:, :, :], attn_w).then_inc(attn_loaded, 16)
            sp.wait_ge(wz_zeroed, 1)
            for g in range(NG):
                sp.dma_start(wz_bd[CG * g:CG * g + CG, CG * g:CG * g + CG], wz_t[g, :, :]).then_inc(wz_loaded, 16)
            sp.dma_start(keys_sb[:, :, :], keys_t).then_inc(keys_loaded, 16)
            sp.dma_start(wq_sb[:, :, :], wq).then_inc(keys_loaded, 16)
            sp.dma_start(last_sb[:, :], last_row).then_inc(last_loaded, 16)
            load(tile_at(0, 1))

            def tile(c, before, after, after2):
                if after2:
                    load(second_after(c))
                if before:
                    store(preceding(c))

            pipeline(tile, sp.Fori)
            store(tile_at(B // 2 - 1, 1))

        @block.gpsimd
        def _(pool):
            for g in range(GROUPS):
                pool.memset(rows[:, GS * g:GS * (g + 1), :], 0.0).then_inc(rows_cleared, 1)
            pool.wait_ge(rows_cleared, GROUPS)

            def tile(c, before, after, after2):
                pool.wait_ge(idx_ready, c.t + 1)
                for g in range(GROUPS):
                    need(pool, rows_used, GROUPS * (c.t - 1) + g + 1)
                    hold(pool, pool_held)
                    for s in range(GS * g, GS * (g + 1)):
                        pool.indirect_dma_start(
                            rows[:, s, :], None, table,
                            bass.IndirectOffsetOnAxis(ap=idx[:, c.par, s:s + 1], axis=0),
                            bounds_check=LAST - 1, oob_is_err=False).then_inc(gathered[g], 16)

            pipeline(tile, pool.Fori)

        @block.vector
        def _(dve):
            attn_chain = Chain(dve, attn_steps, ATTN_STEPS, dve_held)
            ffn_chain = Chain(dve, ffn_steps, FFN_STEPS, dve_held)

            def rsqrt(chain, hv, y, scratch):
                chain.did(dve.tensor_scalar(y.bitcast(I32), hv.bitcast(I32), -0.5, MINUS_GUESS, ALU.mult, ALU.add))
                for k in range(3):
                    chain.settle()
                    chain.did(dve.tensor_scalar(scratch, hv, y, y, ALU.mult, ALU.mult))
                    chain.settle()
                    chain.did(dve.scalar_tensor_tensor(out=y, in0=scratch, scalar=1.5, in1=y, op0=ALU.subtract,
                                                       op1=ALU.mult))
                chain.settle()

            def normed(chain, src, k):
                mean, half_var = mv[:, k, 0:1], sc[:, 8 * k:8 * k + 1]
                rstd = sc[:, 8 * k + 1:8 * k + 2]
                chain.did(dve.bn_stats(bn[:, k, :], src))
                chain.settle_apart()
                chain.did(dve.bn_aggr(mv[:, k, :], bn[:, k, :]))
                chain.settle()
                chain.did(dve.tensor_scalar(half_var, mv[:, k, 1:2], EPS, 0.5, ALU.add, ALU.mult))
                chain.settle()
                rsqrt(chain, half_var, rstd, sc[:, 8 * k + 2:8 * k + 3])
                return mean, rstd

            mean_c, var_c = rowstats[:, 1:2], rowstats[:, 2:3]
            sum_g, mean_g = sc[:, 16:17], sc[:, 17:18]
            dm, q, half_att2, half_var_x, rs_x = (sc[:, k:k + 1] for k in range(18, 23))
            scale_x, shift_x = sc[:, 23:24], sc[:, 24:25]

            def norm_x(n):
                attn_chain.begin(n.t)
                dve.wait_ge(x_loaded[n.par], 32 * (n.half + 1))
                mean, rstd = normed(attn_chain, x_sb[:, n.par, :], 0)
                need(dve, p_ready, n.t)
                dve.tensor_scalar(xn[:, :], x_sb[:, n.par, :], mean, rstd, ALU.subtract, ALU.mult).then_inc(xn_ready, 1)

            def z_stats(n):
                dve.wait_ge(g_copied, n.t + 1)
                attn_chain.did(dve.bn_stats(bn[:, 2, :], ps_gz[:, D:2 * D]))
                dve.scalar_tensor_tensor(out=y_sb[:, :], in0=ctx_sb[:, n.par, :], scalar=gains[:, 0:1],
                                         in1=x_sb[:, n.par, :], op0=ALU.mult, op1=ALU.add).then_inc(xc_used, 1)
                attn_chain.settle_apart()
                dve.bn_aggr(rowstats[:, 1:3], bn[:, 2, :]).then_inc(stats_ready, 1)

            def pg_sums(n):
                dve.wait_ge(p_ready, n.t + 1)
                dve.tensor_tensor_reduce(g_copy[:, :], ps_p[:, 0:D], g_copy[:, :], 1.0, 0.0, ALU.mult, ALU.add,
                                         rowstats[:, 0:1]).then_inc(stats_ready, 1)

            def spread(n):
                dve.wait_ge(avg_ready, 2 * n.t + 1)
                attn_chain.did(dve.tensor_copy(sc[:, 16:18], ps_p[:, STAT:STAT + 2]))
                attn_chain.settle()
                attn_chain.did(dve.tensor_scalar(dm, mean_c, mean_g, None, ALU.subtract))
                attn_chain.settle()
                dve.scalar_tensor_tensor(out=q, in0=dm, scalar=dm, in1=var_c, op0=ALU.mult,
                                         op1=ALU.add).then_inc(q_ready, 1)
                k = (ATT_SCALE * CG) ** 2 / 2
                attn_chain.did(dve.tensor_scalar(half_att2, sum_g, sum_g, k, ALU.mult, ALU.mult))

            def affine(n):
                dve.wait_ge(avg_ready, 2 * n.t + 2)
                attn_chain.settle()
                attn_chain.did(dve.tensor_scalar(half_var_x, ps_p[:, STAT + 2:STAT + 3], half_att2, EPS / 2, ALU.mult, ALU.add))
                attn_chain.settle()
                rsqrt(attn_chain, half_var_x, rs_x, sc[:, 25:26])
                dve.tensor_scalar(scale_x, rs_x, sum_g, gain_gamma[:, :], ALU.mult, ALU.mult).then_inc(affine_ready, 1)
                dve.wait_ge(affine_ready, n.t + 1)
                attn_chain.did(dve.scalar_tensor_tensor(out=shift_x, in0=scale_x, scalar=mean_g, in1=gain_beta[:, :],
                                                   op0=ALU.mult, op1=ALU.subtract))
                attn_chain.end()

            def residual(n):
                dve.wait_ge(att_ready, n.t + 1)
                dve.wait_ge(xc_used, n.t + 1)
                dve.wait_ge(attn_steps, ATTN_STEPS * (n.t + 1))
                ffn_chain.begin(n.t)
                ffn_chain.did(dve.scalar_tensor_tensor(out=x1[:, n.par, :], in0=y_sb[:, :], scalar=shift_x,
                                                   in1=att_out[:, :], op0=ALU.subtract, op1=ALU.add))
                ffn_chain.settle()
                mean, rstd = normed(ffn_chain, x1[:, n.par, :], 1)
                dve.tensor_scalar(h[:, n.par, :], x1[:, n.par, :], mean, rstd, ALU.subtract,
                                  ALU.mult).then_inc(h_ready, 1)
                dve.wait_ge(h_ready, n.t + 1)
                ffn_chain.did(dve.tensor_tensor_reduce(y_sb[:, :], h[:, n.par, :], last_sb[:, 0:D], 1.0, 0.0, ALU.mult,
                                                   ALU.add, dots[:, n.par, 0:1]))

            def key_tops(n):
                def sim(ph):
                    return ps_sim[ph // HEADS][:, NKEYS * (ph % HEADS):NKEYS * (ph % HEADS + 1)]

                for ph in range(NH2):
                    if ph % HEADS == 0:
                        dve.wait_ge(sims_ready, 2 * n.t + ph // HEADS + 1)
                        hold(dve, dve_held)
                    last = dve.max(top[:, ph, :], sim(ph))
                ffn_chain.did(last)
                ffn_chain.settle_apart()
                for ph in range(NH2):
                    last = dve.max_index(top_ix[:, ph, :], top[:, ph, :], sim(ph))
                last.then_inc(sims_used, 1)

            def pair_tops(n):
                ffn_chain.did(dve.tensor_tensor(
                    pair_sum[:, :, :, :],
                    top[:, 0:HEADS, :].unsqueeze(3).broadcast_to([P, HEADS, TOPK, TOPK]),
                    top[:, HEADS:NH2, :].unsqueeze(2).broadcast_to([P, HEADS, TOPK, TOPK]), ALU.add))
                ffn_chain.settle_apart()
                sums = pair_sum[:, :, :, :].rearrange("p h a b -> p h (a b)")
                for hd in range(HEADS):
                    last = dve.max(best[:, hd, :], sums[:, hd, :])
                ffn_chain.did(last)
                ffn_chain.settle_apart()
                for hd in range(HEADS):
                    last = dve.max_index(best_ix[:, TOPK * hd:TOPK * (hd + 1)], best[:, hd, :], sums[:, hd, :])
                ffn_chain.did(last)
                dve.tensor_tensor(shifted[:, :, :], best[:, :, :],
                                  best[:, :, 0:1].broadcast_to([P, HEADS, TOPK]),
                                  ALU.subtract).then_inc(shift_ready, 1)

            def decode(n):
                ffn_chain.settle()
                ffn_chain.did(dve.tensor_scalar(rank[:, 0:SLOTS], best_ix[:, :], 3, None, ALU.logical_shift_right))
                ffn_chain.did(dve.tensor_scalar(rank[:, SLOTS:2 * SLOTS], best_ix[:, :], TOPK - 1, None, ALU.bitwise_and))
                ffn_chain.settle()
                ffn_chain.did(dve.tensor_tensor(onehot[:, :, :],
                                            rank[:, :].unsqueeze(2).broadcast_to([P, NH2 * TOPK, TOPK]),
                                            iota_sb[:, :].unsqueeze(1).broadcast_to([P, NH2 * TOPK, TOPK]),
                                            ALU.is_equal))
                ffn_chain.settle()
                dve.wait_ge(sims_used, n.t + 1)
                ffn_chain.did(dve.tensor_tensor(picked[:, :, :].rearrange("p (f k) a -> p f k a", k=TOPK),
                                            onehot[:, :, :].rearrange("p (f k) a -> p f k a", k=TOPK),
                                            top_ix[:, :, :].unsqueeze(2).broadcast_to([P, NH2, TOPK, TOPK]),
                                            ALU.mult))
                ffn_chain.settle()
                ffn_chain.did(dve.tensor_reduce(key_no[:, :], picked[:, :, :], AX_X, ALU.add))
                ffn_chain.settle()
                dve.scalar_tensor_tensor(out=idx[:, n.par, :], in0=key_no[:, 0:SLOTS], scalar=float(NKEYS),
                                         in1=key_no[:, SLOTS:2 * SLOTS], op0=ALU.mult,
                                         op1=ALU.add).then_inc(idx_ready, 1)

            def weights(n):
                dve.wait_ge(exp_ready, n.t + 1)
                ffn_chain.did(dve.tensor_reduce(exp_sum[:, :], expo[:, :, :], AX_X, ALU.add))
                ffn_chain.settle()
                ffn_chain.did(dve.reciprocal(exp_inv[:, :], exp_sum[:, :]))
                ffn_chain.settle()
                ffn_chain.did(dve.tensor_tensor(prob[:, :].rearrange("p (a k) -> p a k", k=TOPK), expo[:, :, :],
                                            exp_inv[:, :].unsqueeze(2).broadcast_to([P, HEADS, TOPK]), ALU.mult))
                ffn_chain.settle()
                dve.wait_ge(idx_ready, n.t + 1)
                ffn_chain.did(dve.scalar_tensor_tensor(out=clamped[:, :], in0=idx[:, n.par, :], scalar=float(LAST),
                                                   in1=prob[:, :], op0=ALU.is_ge, op1=ALU.mult))
                ffn_chain.did(dve.scalar_tensor_tensor(out=pv[:, n.par, 1:SLOTS + 1], in0=idx[:, n.par, :],
                                                   scalar=float(LAST), in1=prob[:, :], op0=ALU.is_lt, op1=ALU.mult))
                ffn_chain.settle()
                ffn_chain.did(dve.tensor_reduce(pv[:, n.par, 0:1], clamped[:, :], AX_X, ALU.add))
                ffn_chain.settle()
                ffn_chain.end()

            def dot(c, s):
                g = s // GS
                if s % GS == 0:
                    dve.wait_ge(gathered[g], 16 * GS * (c.t + 1))
                made = dve.tensor_tensor_reduce(products[:, s % (2 * GS), :], h[:, c.par, :], rows[:, s, 0:D], 1.0, 0.0, ALU.mult,
                                                ALU.add, dots[:, c.par, 1 + s:2 + s])
                if s % GS == GS - 1:
                    made.then_inc(dots_ready, 1)

            def weigh(c, g):
                a, b = (0 if g == 0 else 1 + GS * g), 1 + GS * (g + 1)
                dve.wait_ge(silu_ready, GROUPS * c.t + g + 1)
                dve.tensor_tensor(w[:, c.par, a:b], silu[:, c.par, a:b], pv[:, c.par, a:b],
                                  ALU.mult).then_inc(w_ready, 1)

            def mlp_gate(c, hf):
                n = 2 * c.t + hf + 1
                dve.wait_ge(up_ready, 2 * n)
                dve.wait_ge(mlp_silu_ready, n)
                need(dve, mt_ps_ready, n - 1)
                dve.tensor_tensor(mlp_m[:, :], mlp_silu[:, :], ps_u[:, :], ALU.mult).then_inc(m_ready, 1)

            def finish(c):
                dve.wait_ge(rows_used, GROUPS * (c.t + 1))
                dve.wait_ge(x1_copied, c.t + 1)
                dve.scalar_tensor_tensor(out=o_sb[:, c.par, :], in0=ps_acc[c.par][:, 0:D],
                                         scalar=gains[:, 1:2], in1=o_sb[:, c.par, :], op0=ALU.mult,
                                         op1=ALU.add).then_inc(out_ready, 1)

            dve.memset(wz_bd[:, :], 0.0).then_inc(wz_zeroed, 1)
            first = tile_at(0, 0)
            norm_x(first)
            dve.wait_ge(wzt_ps_ready, 1)
            dve.tensor_copy(wzt_sb[:, :], ps_acc[0][:, 0:P]).then_inc(wzt_ready, 1)
            dve.wait_ge(gains_ready, 1)
            dve.wait_ge(cols_loaded, 16)
            dve.tensor_scalar(gain_gamma[:, :], cols_sb[:, 0:1], gains[:, 0:1], ATT_SCALE * CG, ALU.mult,
                              ALU.mult).then_inc(setup_dve, 1)
            dve.tensor_scalar(gain_beta[:, :], cols_sb[:, 1:2], gains[:, 0:1], None, ALU.mult).then_inc(setup_dve, 1)
            dve.wait_ge(setup_dve, 2)
            z_stats(first)
            pg_sums(first)
            spread(first)
            affine(first)
            dve.wait_ge(last_loaded, 16)
            residual(first)
            key_tops(first)
            pair_tops(first)
            dve.wait_ge(consts_loaded, 32)
            decode(first)
            weights(first)
            second = tile_at(0, 1)
            norm_x(second)
            z_stats(second)
            pg_sums(second)
            spread(second)
            affine(second)

            def dots_of(c, first_slot, end_slot):
                for s in range(first_slot, end_slot):
                    dot(c, s)

            def tile(c, before, after, after2):
                b, n, m = preceding(c), following(c), second_after(c)
                if before:
                    weigh(b, GROUPS - 1)
                if after:
                    residual(n)
                dots_of(c, 0, 6)
                weigh(c, 0)
                dots_of(c, 6, 8)
                if after:
                    key_tops(n)
                mlp_gate(c, 0)
                weigh(c, 1)
                if after:
                    pair_tops(n)
                if before:
                    finish(b)
                dots_of(c, 8, 12)
                if after:
                    decode(n)
                weigh(c, 2)
                dots_of(c, 12, 16)
                if after:
                    weights(n)
                weigh(c, 3)
                if after2:
                    norm_x(m)
                dots_of(c, 16, 20)
                if after2:
                    z_stats(m)
                weigh(c, 4)
                dots_of(c, 20, 22)
                if after2:
                    pg_sums(m)
                mlp_gate(c, 1)
                dots_of(c, 22, 28)
                weigh(c, 5)
                if after2:
                    spread(m)
                dots_of(c, 28, 30)
                weigh(c, 6)
                if after2:
                    affine(m)
                dots_of(c, 30, 32)

            pipeline(tile, dve.Fori)
            end = tile_at(B // 2 - 1, 1)
            weigh(end, GROUPS - 1)
            finish(end)

        @block.scalar
        def _(act):
            act.dma_start(cols_sb[:, :], cols).then_inc(cols_loaded, 16)
            act.dma_start(consts_sb[:, :, :], consts).then_inc(consts_loaded, 16)
            act.dma_start(iota_sb[:, :], iota8).then_inc(consts_loaded, 16)
            act.dma_start(wg_sb[:, :, :], wg_t).then_inc(mlp_loaded, 16)
            act.dma_start(wu_sb[:, :, :], wu_t).then_inc(mlp_loaded, 16)
            act.dma_start(wd_sb[:, :, :], wd_t).then_inc(mlp_loaded, 16)

            def copy_g(n):
                act.wait_ge(gz_ready, n.t + 1)
                need(act, stats_ready, 2 * n.t)
                act.activation(g_copy[:, :], ps_gz[:, 0:D], ACT.Copy).then_inc(g_copied, 1)

            def scale_z(n):
                act.wait_ge(affine_ready, n.t + 1)
                need(act, h_ready, n.t)
                act.activation(att_out[:, :], ps_gz[:, D:2 * D], ACT.Copy, scale=sc[:, 23:24]).then_inc(att_ready, 1)

            def copy_ht(n):
                act.wait_ge(ht_ps_ready, n.t + 1)
                act.activation(h_t[:, n.par, :, :].rearrange("p k t -> p (k t)"), ps_p[:, 0:D],
                               ACT.Copy).then_inc(ht_ready, 1)

            def exps(n):
                act.wait_ge(shift_ready, n.t + 1)
                act.activation(expo[:, :, :], shifted[:, :, :], ACT.Exp).then_inc(exp_ready, 1)

            def silu_dots(c, g):
                a, b = (0 if g == 0 else 1 + GS * g), 1 + GS * (g + 1)
                act.wait_ge(dots_ready, GROUPS * c.t + g + 1)
                act.activation(silu[:, c.par, a:b], dots[:, c.par, a:b], ACT.Silu).then_inc(silu_ready, 1)

            def diags(c, g):
                act.wait_ge(w_ready, GROUPS * c.t + g + 1)
                need(act, rows_used, GROUPS * c.t + g + 1 - DIAGS)
                for j in range(0 if g == 0 else 1, GS + 1):
                    made = act.activation(diag[:, g % DIAGS, j, :], ident, ACT.Copy,
                                          scale=w[:, c.par, GS * g + j:GS * g + j + 1])
                made.then_inc(diag_ready, 1)

            def mlp_silu_of(c, hf):
                n = 2 * c.t + hf + 1
                act.wait_ge(up_ready, 2 * n - 1)
                need(act, m_ready, n - 1)
                act.activation(mlp_silu[:, :], ps_a[:, :], ACT.Silu).then_inc(mlp_silu_ready, 1)

            def copy_mt(c, hf):
                act.wait_ge(mt_ps_ready, 2 * c.t + hf + 1)
                act.activation(m_t[:, hf, :, :].rearrange("p k t -> p (k t)"), ps_t[:, :],
                               ACT.Copy).then_inc(mt_ready, 1)

            def copy_x1(c):
                act.wait_ge(h_ready, c.t + 1)
                need(act, stored, 16 * c.t)
                act.activation(o_sb[:, c.par, :], x1[:, c.par, :], ACT.Copy).then_inc(x1_copied, 1)

            first = tile_at(0, 0)
            act.wait_ge(cols_loaded, 16)
            act.activation(gains[:, :], cols_sb[:, 2:4], ACT.Tanh).then_inc(gains_ready, 1)
            copy_g(first)
            act.wait_ge(wk_ps_ready, 1)
            wk_flat = wk_sb[:, :, :].rearrange("p k n -> p (k n)")
            for q, src in enumerate((ps_sim[0], ps_sim[1], ps_a, ps_u)):
                act.activation(wk_flat[:, 512 * q:512 * (q + 1)], src[:, :], ACT.Copy).then_inc(wk_ready, 1)
            scale_z(first)
            copy_ht(first)
            exps(first)
            act.wait_ge(consts_loaded, 32)
            copy_g(tile_at(0, 1))
            scale_z(tile_at(0, 1))

            def tile(c, before, after, after2):
                b, n, m = preceding(c), following(c), second_after(c)
                if before:
                    diags(b, GROUPS - 1)
                if after:
                    copy_ht(n)
                mlp_silu_of(c, 0)
                silu_dots(c, 0)
                diags(c, 0)
                silu_dots(c, 1)
                diags(c, 1)
                copy_mt(c, 0)
                if after:
                    exps(n)
                silu_dots(c, 2)
                diags(c, 2)
                mlp_silu_of(c, 1)
                silu_dots(c, 3)
                copy_x1(c)
                diags(c, 3)
                if after2:
                    copy_g(m)
                silu_dots(c, 4)
                diags(c, 4)
                silu_dots(c, 5)
                copy_mt(c, 1)
                silu_dots(c, 6)
                diags(c, 5)
                diags(c, 6)
                if after2:
                    scale_z(m)
                silu_dots(c, 7)

            pipeline(tile, act.Fori)
            diags(tile_at(B // 2 - 1, 1), GROUPS - 1)

        @block.tensor
        def _(pe):
            def attn_gz(n):
                pe.wait_ge(x_loaded[n.par], 32 * (n.half + 1))
                need(pe, att_ready, n.t)
                pe.matmul(ps_gz[:, 0:D], wg_attn, ctx_sb[:, n.par, :], start=True, stop=True)
                pe.matmul(ps_gz[:, D:2 * D], wzt_sb[:, :], ctx_sb[:, n.par, :], start=True,
                          stop=True).then_inc(gz_ready, 1)

            def attn_p(n):
                pe.wait_ge(xn_ready, n.t + 1)
                need(pe, ht_ready, n.t)
                pe.matmul(ps_p[:, 0:D], wp_attn, xn[:, :], start=True, stop=True).then_inc(p_ready, 1)

            def group_means(n):
                pe.wait_ge(stats_ready, 2 * n.t + 2)
                pe.matmul(ps_p[:, STAT:STAT + 2], group_mean, rowstats[:, 0:2], start=True,
                          stop=True).then_inc(avg_ready, 1)

            def group_var(n):
                pe.wait_ge(q_ready, n.t + 1)
                pe.matmul(ps_p[:, STAT + 2:STAT + 3], group_mean, sc[:, 19:20], start=True,
                          stop=True).then_inc(avg_ready, 1)

            def turn_h(n):
                pe.wait_ge(h_ready, n.t + 1)
                for kt in range(KT):
                    last = pe.transpose(ps_p[:, P * kt:P * (kt + 1)], h[:, n.par, P * kt:P * (kt + 1)], ident)
                last.then_inc(ht_ps_ready, 1)

            def sims(n):
                pe.wait_ge(ht_ready, n.t + 1)
                need(pe, sims_used, n.t)
                for f in range(2):
                    for kt in range(KT):
                        last = pe.matmul(ps_sim[f][:, :], h_t[:, n.par, kt, :], wk_sb[:, kt, 512 * f:512 * (f + 1)],
                                         start=(kt == 0), stop=(kt == KT - 1))
                    last.then_inc(sims_ready, 1)

            def mlp_up(c, hf, bank_, weights_):
                need(pe, mt_ready, 2 * c.t + hf)
                for kt in range(KT):
                    last = pe.matmul(bank_[:, :], h_t[:, c.par, kt, :], weights_[:, kt, HALF * hf:HALF * (hf + 1)],
                                     start=(kt == 0), stop=(kt == KT - 1))
                last.then_inc(up_ready, 1)

            def mlp_turn(c, hf):
                pe.wait_ge(m_ready, 2 * c.t + hf + 1)
                for q in range(HC):
                    turned = pe.transpose(ps_t[:, P * q:P * (q + 1)], mlp_m[:, P * q:P * (q + 1)], ident)
                turned.then_inc(mt_ps_ready, 1)

            def mlp_down(c, hf):
                pe.wait_ge(mt_ready, 2 * c.t + hf + 1)
                for q in range(HC):
                    pe.matmul(ps_acc[c.par][:, 0:D], m_t[:, hf, q, :], wd_sb[:, HC * hf + q, :],
                              start=False, stop=False)

            def experts(c, g):
                pe.wait_ge(diag_ready, GROUPS * c.t + g + 1)
                if g == 0:
                    need(pe, out_ready, c.t - 1)
                for j in range(0 if g == 0 else 1, GS + 1):
                    s = GS * g + j
                    up = last_sb[:, D:2 * D] if s == 0 else rows[:, s - 1, D:2 * D]
                    last = pe.matmul(ps_acc[c.par][:, 0:D], diag[:, g % DIAGS, j, :], up,
                                     start=(s == 0), stop=(s == SLOTS))
                last.then_inc(rows_used, 1)

            pe.wait_ge(attn_loaded, 16)
            pe.wait_ge(wz_loaded, 16 * NG)
            pe.matmul(ps_acc[0][:, 0:P], wt_attn, wz_bd[:, :], start=True, stop=True).then_inc(wzt_ps_ready, 1)
            first = tile_at(0, 0)
            attn_p(first)
            pe.wait_ge(wzt_ready, 1)
            attn_gz(first)
            pe.wait_ge(keys_loaded, 32)
            wk_banks = (ps_sim[0], ps_sim[1], ps_a, ps_u)
            for kt in range(KT):
                for ph in range(NH2):
                    at = NH2 * kt + ph
                    last = pe.matmul(wk_banks[at // 4][:, NKEYS * (at % 4):NKEYS * (at % 4 + 1)],
                                     wq_sb[:, ph, P * kt:P * (kt + 1)], keys_sb[:, ph, :], start=True, stop=True)
            last.then_inc(wk_ps_ready, 1)
            pe.wait_ge(consts_loaded, 32)
            group_means(first)
            group_var(first)
            turn_h(first)
            pe.wait_ge(wk_ready, 4)
            sims(first)
            second = tile_at(0, 1)
            attn_gz(second)
            attn_p(second)
            group_means(second)
            group_var(second)
            pe.wait_ge(mlp_loaded, 48)

            def tile(c, before, after, after2):
                b, n, m = preceding(c), following(c), second_after(c)
                mlp_up(c, 0, ps_a, wg_sb)
                if after:
                    turn_h(n)
                if after2:
                    attn_gz(m)
                if after:
                    sims(n)
                mlp_up(c, 0, ps_u, wu_sb)
                if before:
                    experts(b, GROUPS - 1)
                mlp_turn(c, 0)
                experts(c, 0)
                mlp_up(c, 1, ps_a, wg_sb)
                experts(c, 1)
                mlp_down(c, 0)
                mlp_up(c, 1, ps_u, wu_sb)
                experts(c, 2)
                if after2:
                    attn_p(m)
                experts(c, 3)
                if after2:
                    group_means(m)
                mlp_turn(c, 1)
                experts(c, 4)
                if after2:
                    group_var(m)
                mlp_down(c, 1)
                experts(c, 5)
                experts(c, 6)

            pipeline(tile, pe.Fori)
            experts(tile_at(B // 2 - 1, 1), GROUPS - 1)


def kernel(**inputs):
    import numpy as np
    import concourse.bacc as bacc
    from concourse import mybir as _mybir
    from concourse.bass_utils import run_bass_kernel_spmd

    a = {k: np.asarray(v) for k, v in inputs.items()}
    x = a["x"]
    b, c, d = x.shape
    heads, nkeys, _, kn = a["L0_ffn_keys"].shape
    inter = a["L0_ffn_Wg"].shape[0]
    kt = d // c
    cg = a["L0_xattn_Wz"].shape[1]
    table = np.concatenate([a["L0_ffn_down_embed"], a["L0_ffn_up_embed"]], axis=1)
    consts = np.zeros((c, 2, c), np.float32)
    consts[:, 0, :] = np.eye(c, dtype=np.float32)
    consts[:, 1, :] = np.kron(np.eye(c // cg, dtype=np.float32), np.full((cg, cg), 1.0 / cg, np.float32))
    laid = [
        ("x", x),
        ("ctx", a["ctx_1024"]),
        ("attn_w", np.stack([a["L0_xattn_Wp"].T, a["L0_xattn_Wg"].T, a["L0_xattn_Wt"]], axis=1)),
        ("wz_t", a["L0_xattn_Wz"].transpose(0, 2, 1)),
        ("cols", np.stack([a["L0_xattn_gamma"], a["L0_xattn_beta"],
                           np.broadcast_to(a["g_xattn"], (c,)), np.broadcast_to(a["g_ffn"], (c,))], axis=1)),
        ("wq", a["L0_ffn_Wq"].reshape(2 * heads, kn, d).transpose(1, 0, 2)),
        ("keys_t", a["L0_ffn_keys"].transpose(3, 2, 0, 1).reshape(kn, 2 * heads, nkeys)),
        ("table", table),
        ("last_row", np.broadcast_to(table[-1], (c, 2 * d))),
        ("wg_t", a["L0_ffn_Wg"].T.reshape(kt, c, inter).transpose(1, 0, 2)),
        ("wu_t", a["L0_ffn_Wu"].T.reshape(kt, c, inter).transpose(1, 0, 2)),
        ("wd_t", a["L0_ffn_Wd"].T.reshape(inter // c, c, d).transpose(1, 0, 2)),
        ("consts", consts),
        ("iota8", np.tile(np.arange(8, dtype=np.uint16), (c, 1))),
    ]
    nc = bacc.Bacc("TRN2", target_bir_lowering=False, num_devices=1)
    arrays, args = {}, []
    for name, value in laid:
        value = np.ascontiguousarray(value)
        arrays[f"in_{name}"] = value
        args.append(nc.dram_tensor(f"in_{name}", value.shape, _mybir.dt.from_np(value.dtype), kind="ExternalInput").ap())
    args.append(nc.dram_tensor("out_y", x.shape, _mybir.dt.float32, kind="ExternalOutput").ap())
    gated_block(nc, *args)
    return run_bass_kernel_spmd(nc, [arrays], core_ids=[0]).results[0]["out_y"]
```

```python
from collections import namedtuple
from contextlib import ExitStack

import concourse.bass as bass
from concourse import mybir

F32 = mybir.dt.float32
BF16 = mybir.dt.bfloat16
I32 = mybir.dt.int32
U16 = mybir.dt.uint16
ALU = mybir.AluOpType
ACT = mybir.ActivationFunctionType
AX_X = mybir.AxisListType.X

P = 128
TOPK = 8
EPS = 1e-5
ATT_SCALE = 0.125
MINUS_GUESS = float(0x5F3759DF - (1 << 22) - (1 << 31))

Tile = namedtuple("Tile", "t par half")


def tile_at(pair, k):
    return Tile(2 * pair + k, k % 2, pair + k // 2)


def need(eng, sem, value):
    if not (isinstance(value, int) and value <= 0):
        eng.wait_ge(sem, value)


def hold(eng, sem):
    eng.sem_inc(sem, 1)


class Chain:

    def __init__(self, eng, sem, per_tile, held):
        self.eng, self.sem, self.per_tile, self.held = eng, sem, per_tile, held
        self.beside = None

    def begin(self, t):
        self.base, self.n = t * self.per_tile, 0

    def did(self, instruction):
        instruction.then_inc(self.sem, 1)
        self.n += 1

    def settle(self):
        if self.beside:
            self.beside()
        self.eng.wait_ge(self.sem, self.base + self.n)

    def settle_apart(self):
        self.settle()
        hold(self.eng, self.held)

    def end(self):
        assert self.n == self.per_tile, self.n


def gated_block(nc, x, ctx, attn_w, cols, wq, keys_t, table, last_row, wg_t, wu_t, wd_t,
                consts, iota8, CG, out):
    B, _, D = x.shape
    HEADS = keys_t.shape[1] // 2
    NH2 = 2 * HEADS
    KN = wq.shape[0]
    NKEYS = keys_t.shape[2]
    INTER = wg_t.shape[2]
    KT = D // P
    HALF = INTER // 2
    HC = HALF // P
    SLOTS = HEADS * TOPK
    GS = 4
    GROUPS = SLOTS // GS
    LAST = table.shape[0] - 1
    DIAGS = 4
    ATTN_STEPS, FFN_STEPS = 23, 27
    assert GROUPS == 8

    with ExitStack() as stack:
        def sb(name, shape, dt=F32):
            return stack.enter_context(nc.sbuf_tensor(name, shape, dt))

        def bank(name):
            return stack.enter_context(nc.psum_tensor(name, [P, 512], F32))

        def sem(name):
            return stack.enter_context(nc.semaphore(name))

        attn_sb = sb("attn_sb", [P, 4, P])
        wzt_sb = sb("wzt_sb", [P, P])
        cols_sb = sb("cols_sb", [P, 4])
        gains = sb("gains", [P, 2])
        gain_gamma = sb("gain_gamma", [P, 1])
        gain_beta = sb("gain_beta", [P, 1])
        wq_sb = sb("wq_sb", [KN, NH2, D])
        keys_sb = sb("keys_sb", [KN, NH2, NKEYS])
        wk_sb = sb("wk_sb", [P, KT, NH2 * NKEYS])
        last_sb = sb("last_sb", [P, 2 * D])
        wg_sb = sb("wg_sb", [P, KT, INTER])
        wu_sb = sb("wu_sb", [P, KT, INTER])
        wd_sb = sb("wd_sb", [P, INTER // P, D])
        consts_sb = sb("consts_sb", [P, 2, P])
        iota_sb = sb("iota_sb", [P, TOPK], U16)
        ident = consts_sb[:, 0, :]
        group_mean = consts_sb[:, 1, :]
        wp_attn, wg_attn, wt_attn, wz_attn = (attn_sb[:, k, :] for k in range(4))

        x_sb = sb("x_sb", [P, 2, D])
        ctx_sb = sb("ctx_sb", [P, 2, D])
        x1 = sb("x1", [P, 2, D])
        h = sb("h", [P, 2, D])
        h_t = sb("h_t", [P, 2, KT, P])
        idx = sb("idx", [P, 2, SLOTS], I32)
        pv = sb("pv", [P, 2, SLOTS + 1])
        dots = sb("dots", [P, 2, SLOTS + 1])
        silu = sb("silu", [P, 2, SLOTS + 1])
        w = sb("w", [P, 2, SLOTS + 1])
        o_sb = sb("o_sb", [P, 2, D])
        xn = sb("xn", [P, D])
        g_copy = sb("g_copy", [P, D])
        y_sb = sb("y_sb", [P, D])
        att_out = sb("att_out", [P, D])
        products = sb("products", [P, 2 * GS, D])
        bn = sb("bn", [P, 3, 6])
        mv = sb("mv", [P, 2, 2])
        rowstats = sb("rowstats", [P, 3])
        sc = sb("sc", [P, 32])
        top = sb("top", [P, NH2, TOPK])
        top_ix = sb("top_ix", [P, NH2, TOPK], U16)
        pair_sum = sb("pair_sum", [P, HEADS, TOPK, TOPK])
        best = sb("best", [P, HEADS, TOPK])
        best_ix = sb("best_ix", [P, SLOTS], U16)
        rank = sb("rank", [P, NH2 * TOPK], U16)
        onehot = sb("onehot", [P, NH2 * TOPK, TOPK], BF16)
        picked = sb("picked", [P, NH2 * TOPK, TOPK], BF16)
        key_no = sb("key_no", [P, NH2 * TOPK])
        shifted = sb("shifted", [P, HEADS, TOPK])
        expo = sb("expo", [P, HEADS, TOPK])
        exp_sum = sb("exp_sum", [P, HEADS])
        exp_inv = sb("exp_inv", [P, HEADS])
        prob = sb("prob", [P, SLOTS])
        clamped = sb("clamped", [P, SLOTS])
        mlp_silu = sb("mlp_silu", [P, HALF])
        mlp_m = sb("mlp_m", [P, HALF])
        m_t = sb("m_t", [P, 2, HC, P])
        rows = sb("rows", [P, SLOTS, 2 * D])
        diag = sb("diag", [P, DIAGS, GS + 1, P])

        ps_p = bank("ps_p")
        ps_gz = bank("ps_gz")
        ps_sim = [bank("ps_sim0"), bank("ps_sim1")]
        ps_a = bank("ps_a")
        ps_u = bank("ps_u")
        ps_t = ps_a
        ps_acc = [bank("ps_acc0"), bank("ps_acc1")]
        STAT = D

        x_loaded = [sem("x_loaded0"), sem("x_loaded1")]
        attn_loaded = sem("attn_loaded")
        cols_loaded = sem("cols_loaded")
        keys_loaded = sem("keys_loaded")
        last_loaded = sem("last_loaded")
        mlp_loaded = sem("mlp_loaded")
        consts_loaded = sem("consts_loaded")
        stored = sem("stored")
        gains_ready = sem("gains_ready")
        setup_dve = sem("setup_dve")
        wzt_ps_ready = sem("wzt_ps_ready")
        wzt_ready = sem("wzt_ready")
        wk_ps_ready = sem("wk_ps_ready")
        wk_ready = sem("wk_ready")
        attn_steps = sem("attn_steps")
        ffn_steps = sem("ffn_steps")
        dve_held = sem("dve_held")
        pool_held = sem("pool_held")
        sp_held = sem("sp_held")
        xn_ready = sem("xn_ready")
        gz_ready = sem("gz_ready")
        p_ready = sem("p_ready")
        g_copied = sem("g_copied")
        stats_ready = sem("stats_ready")
        avg_ready = sem("avg_ready")
        q_ready = sem("q_ready")
        xc_used = sem("xc_used")
        affine_ready = sem("affine_ready")
        att_ready = sem("att_ready")
        h_ready = sem("h_ready")
        ht_ps_ready = sem("ht_ps_ready")
        ht_ready = sem("ht_ready")
        sims_ready = sem("sims_ready")
        sims_used = sem("sims_used")
        idx_ready = sem("idx_ready")
        shift_ready = sem("shift_ready")
        exp_ready = sem("exp_ready")
        gathered = [sem(f"gathered{g}") for g in range(GROUPS)]
        dots_ready = sem("dots_ready")
        silu_ready = sem("silu_ready")
        w_ready = sem("w_ready")
        diag_ready = sem("diag_ready")
        rows_cleared = sem("rows_cleared")
        rows_used = sem("rows_used")
        up_ready = sem("up_ready")
        mlp_silu_ready = sem("mlp_silu_ready")
        m_ready = sem("m_ready")
        mt_ps_ready = sem("mt_ps_ready")
        mt_ready = sem("mt_ready")
        x1_copied = sem("x1_copied")
        out_ready = sem("out_ready")

        block = stack.enter_context(nc.Block())

        def pipeline(tile, loop, last_tile=None):
            tile(tile_at(0, 0), False, True, True)
            tile(tile_at(0, 1), True, True, True)
            with loop(1, B // 2 - 1) as i:
                tile(tile_at(i, 0), True, True, True)
                tile(tile_at(i, 1), True, True, True)
            tile(tile_at(B // 2 - 1, 0), True, True, False)
            if last_tile is None:
                tile(tile_at(B // 2 - 1, 1), True, False, False)
            else:
                last_tile(tile_at(B // 2 - 1, 1))

        def following(c):
            return Tile(c.t + 1, 1 - c.par, c.half + c.par)

        def second_after(c):
            return Tile(c.t + 2, c.par, c.half + 1)

        def preceding(c):
            return Tile(c.t - 1, 1 - c.par, c.half - (1 - c.par))

        @block.sync
        def _(sp):
            def load(c):
                need(sp, xc_used, c.t - 1)
                sp.dma_start(x_sb[:, c.par, :], x[c.t, :, :]).then_inc(x_loaded[c.par], 16)
                sp.dma_start(ctx_sb[:, c.par, :], ctx[c.t, :, :]).then_inc(x_loaded[c.par], 16)

            def store(c):
                sp.wait_ge(out_ready, c.t + 1)
                sp.dma_start(out[c.t, :, :], o_sb[:, c.par, :]).then_inc(stored, 16)
                sp.wait_ge(stored, 16 * (c.t + 1))
                hold(sp, sp_held)

            load(tile_at(0, 0))
            sp.dma_start(attn_sb[:, :, :], attn_w).then_inc(attn_loaded, 16)
            sp.dma_start(keys_sb[:, :, :], keys_t).then_inc(keys_loaded, 16)
            sp.dma_start(wq_sb[:, :, :], wq).then_inc(keys_loaded, 16)
            sp.dma_start(last_sb[:, :], last_row).then_inc(last_loaded, 16)
            load(tile_at(0, 1))
            sp.dma_start(wg_sb[:, :, :], wg_t).then_inc(mlp_loaded, 16)
            sp.dma_start(wu_sb[:, :, :], wu_t).then_inc(mlp_loaded, 16)
            sp.dma_start(wd_sb[:, :, :], wd_t).then_inc(mlp_loaded, 16)

            def tile(c, before, after, after2):
                if after2:
                    load(second_after(c))
                if before:
                    store(preceding(c))

            pipeline(tile, sp.Fori)
            store(tile_at(B // 2 - 1, 1))

        @block.gpsimd
        def _(pool):
            for g in range(GROUPS):
                pool.memset(rows[:, GS * g:GS * (g + 1), :], 0.0).then_inc(rows_cleared, 1)
            pool.wait_ge(rows_cleared, GROUPS)

            def tile(c, before, after, after2):
                pool.wait_ge(idx_ready, c.t + 1)
                for g in range(GROUPS):
                    need(pool, rows_used, GROUPS * (c.t - 1) + g + 1)
                    hold(pool, pool_held)
                    for s in range(GS * g, GS * (g + 1)):
                        pool.indirect_dma_start(
                            rows[:, s, :], None, table,
                            bass.IndirectOffsetOnAxis(ap=idx[:, c.par, s:s + 1], axis=0),
                            bounds_check=LAST - 1, oob_is_err=False).then_inc(gathered[g], 16)

            pipeline(tile, pool.Fori)

        @block.vector
        def _(dve):
            attn_chain = Chain(dve, attn_steps, ATTN_STEPS, dve_held)
            ffn_chain = Chain(dve, ffn_steps, FFN_STEPS, dve_held)

            def rsqrt(chain, hv, y, scratch):
                chain.did(dve.tensor_scalar(y.bitcast(I32), hv.bitcast(I32), -0.5, MINUS_GUESS, ALU.mult, ALU.add))
                for k in range(3):
                    chain.settle()
                    chain.did(dve.tensor_scalar(scratch, hv, y, y, ALU.mult, ALU.mult))
                    chain.settle()
                    chain.did(dve.scalar_tensor_tensor(out=y, in0=scratch, scalar=1.5, in1=y, op0=ALU.subtract,
                                                       op1=ALU.mult))
                chain.settle()

            def normed(chain, src, k):
                mean, half_var = mv[:, k, 0:1], sc[:, 8 * k:8 * k + 1]
                rstd = sc[:, 8 * k + 1:8 * k + 2]
                chain.did(dve.bn_stats(bn[:, k, :], src))
                chain.settle_apart()
                chain.did(dve.bn_aggr(mv[:, k, :], bn[:, k, :]))
                chain.settle()
                chain.did(dve.tensor_scalar(half_var, mv[:, k, 1:2], EPS, 0.5, ALU.add, ALU.mult))
                chain.settle()
                rsqrt(chain, half_var, rstd, sc[:, 8 * k + 2:8 * k + 3])
                return mean, rstd

            mean_c, var_c = rowstats[:, 1:2], rowstats[:, 2:3]
            sum_g, mean_g = sc[:, 16:17], sc[:, 17:18]
            dm, q, half_att2, half_var_x, rs_x = (sc[:, k:k + 1] for k in range(18, 23))
            scale_x, shift_x = sc[:, 23:24], sc[:, 24:25]

            def norm_x(n):
                attn_chain.begin(n.t)
                dve.wait_ge(x_loaded[n.par], 32 * (n.half + 1))
                mean, rstd = normed(attn_chain, x_sb[:, n.par, :], 0)
                need(dve, p_ready, n.t)
                dve.tensor_scalar(xn[:, :], x_sb[:, n.par, :], mean, rstd, ALU.subtract, ALU.mult).then_inc(xn_ready, 1)

            def z_stats(n):
                dve.wait_ge(g_copied, n.t + 1)
                attn_chain.did(dve.bn_stats(bn[:, 2, :], ps_gz[:, D:2 * D]))
                dve.scalar_tensor_tensor(out=y_sb[:, :], in0=ctx_sb[:, n.par, :], scalar=gains[:, 0:1],
                                         in1=x_sb[:, n.par, :], op0=ALU.mult, op1=ALU.add).then_inc(xc_used, 1)
                attn_chain.settle_apart()
                dve.bn_aggr(rowstats[:, 1:3], bn[:, 2, :]).then_inc(stats_ready, 1)

            def pg_sums(n):
                dve.wait_ge(p_ready, n.t + 1)
                dve.tensor_tensor_reduce(g_copy[:, :], ps_p[:, 0:D], g_copy[:, :], 1.0, 0.0, ALU.mult, ALU.add,
                                         rowstats[:, 0:1]).then_inc(stats_ready, 1)

            def spread(n):
                dve.wait_ge(avg_ready, 2 * n.t + 1)
                attn_chain.did(dve.tensor_copy(sc[:, 16:18], ps_p[:, STAT:STAT + 2]))
                attn_chain.settle()
                attn_chain.did(dve.tensor_scalar(dm, mean_c, mean_g, None, ALU.subtract))
                attn_chain.settle()
                dve.scalar_tensor_tensor(out=q, in0=dm, scalar=dm, in1=var_c, op0=ALU.mult,
                                         op1=ALU.add).then_inc(q_ready, 1)
                k = (ATT_SCALE * CG) ** 2 / 2
                attn_chain.did(dve.tensor_scalar(half_att2, sum_g, sum_g, k, ALU.mult, ALU.mult))

            def affine(n):
                dve.wait_ge(avg_ready, 2 * n.t + 2)
                attn_chain.settle()
                attn_chain.did(dve.tensor_scalar(half_var_x, ps_p[:, STAT + 2:STAT + 3], half_att2, EPS / 2, ALU.mult, ALU.add))
                attn_chain.settle()
                rsqrt(attn_chain, half_var_x, rs_x, sc[:, 25:26])
                dve.tensor_scalar(scale_x, rs_x, sum_g, gain_gamma[:, :], ALU.mult, ALU.mult).then_inc(affine_ready, 1)
                dve.wait_ge(affine_ready, n.t + 1)
                attn_chain.did(dve.scalar_tensor_tensor(out=shift_x, in0=scale_x, scalar=mean_g, in1=gain_beta[:, :],
                                                   op0=ALU.mult, op1=ALU.subtract))
                attn_chain.end()

            def residual(n):
                dve.wait_ge(att_ready, n.t + 1)
                dve.wait_ge(xc_used, n.t + 1)
                need(dve, x1_copied, n.t - 1)
                dve.wait_ge(attn_steps, ATTN_STEPS * (n.t + 1))
                ffn_chain.begin(n.t)
                ffn_chain.did(dve.scalar_tensor_tensor(out=x1[:, n.par, :], in0=y_sb[:, :], scalar=shift_x,
                                                   in1=att_out[:, :], op0=ALU.subtract, op1=ALU.add))

            def norm_h(n):
                ffn_chain.settle()
                mean, rstd = normed(ffn_chain, x1[:, n.par, :], 1)
                dve.tensor_scalar(h[:, n.par, :], x1[:, n.par, :], mean, rstd, ALU.subtract,
                                  ALU.mult).then_inc(h_ready, 1)
                dve.wait_ge(h_ready, n.t + 1)
                ffn_chain.did(dve.tensor_tensor_reduce(y_sb[:, :], h[:, n.par, :], last_sb[:, 0:D], 1.0, 0.0, ALU.mult,
                                                   ALU.add, dots[:, n.par, 0:1]))

            def sim(ph):
                return ps_sim[ph // HEADS][:, NKEYS * (ph % HEADS):NKEYS * (ph % HEADS + 1)]

            def key_tops0(n):
                dve.wait_ge(sims_ready, 2 * n.t + 1)
                hold(dve, dve_held)
                for ph in range(HEADS):
                    dve.max(top[:, ph, :], sim(ph))

            def key_tops1(n):
                dve.wait_ge(sims_ready, 2 * n.t + 2)
                hold(dve, dve_held)
                for ph in range(HEADS, NH2):
                    last = dve.max(top[:, ph, :], sim(ph))
                ffn_chain.did(last)
                ffn_chain.settle_apart()
                for ph in range(NH2):
                    last = dve.max_index(top_ix[:, ph, :], top[:, ph, :], sim(ph))
                last.then_inc(sims_used, 1)

            def pair_tops(n):
                ffn_chain.did(dve.tensor_tensor(
                    pair_sum[:, :, :, :],
                    top[:, 0:HEADS, :].unsqueeze(3).broadcast_to([P, HEADS, TOPK, TOPK]),
                    top[:, HEADS:NH2, :].unsqueeze(2).broadcast_to([P, HEADS, TOPK, TOPK]), ALU.add))
                ffn_chain.settle_apart()
                sums = pair_sum[:, :, :, :].rearrange("p h a b -> p h (a b)")
                for hd in range(HEADS):
                    last = dve.max(best[:, hd, :], sums[:, hd, :])
                ffn_chain.did(last)
                ffn_chain.settle_apart()
                for hd in range(HEADS):
                    last = dve.max_index(best_ix[:, TOPK * hd:TOPK * (hd + 1)], best[:, hd, :], sums[:, hd, :])
                ffn_chain.did(last)
                dve.tensor_tensor(shifted[:, :, :], best[:, :, :],
                                  best[:, :, 0:1].broadcast_to([P, HEADS, TOPK]),
                                  ALU.subtract).then_inc(shift_ready, 1)

            def decode(n):
                ffn_chain.settle()
                ffn_chain.did(dve.tensor_scalar(rank[:, 0:SLOTS], best_ix[:, :], 3, None, ALU.logical_shift_right))
                ffn_chain.did(dve.tensor_scalar(rank[:, SLOTS:2 * SLOTS], best_ix[:, :], TOPK - 1, None, ALU.bitwise_and))
                ffn_chain.settle()
                ffn_chain.did(dve.tensor_tensor(onehot[:, :, :],
                                            rank[:, :].unsqueeze(2).broadcast_to([P, NH2 * TOPK, TOPK]),
                                            iota_sb[:, :].unsqueeze(1).broadcast_to([P, NH2 * TOPK, TOPK]),
                                            ALU.is_equal))
                ffn_chain.settle()
                dve.wait_ge(sims_used, n.t + 1)
                ffn_chain.did(dve.tensor_tensor(picked[:, :, :].rearrange("p (f k) a -> p f k a", k=TOPK),
                                            onehot[:, :, :].rearrange("p (f k) a -> p f k a", k=TOPK),
                                            top_ix[:, :, :].unsqueeze(2).broadcast_to([P, NH2, TOPK, TOPK]),
                                            ALU.mult))
                ffn_chain.settle()
                ffn_chain.did(dve.tensor_reduce(key_no[:, :], picked[:, :, :], AX_X, ALU.add))
                ffn_chain.settle()
                dve.scalar_tensor_tensor(out=idx[:, n.par, :], in0=key_no[:, 0:SLOTS], scalar=float(NKEYS),
                                         in1=key_no[:, SLOTS:2 * SLOTS], op0=ALU.mult,
                                         op1=ALU.add).then_inc(idx_ready, 1)

            def weights(n):
                dve.wait_ge(exp_ready, n.t + 1)
                ffn_chain.did(dve.tensor_reduce(exp_sum[:, :], expo[:, :, :], AX_X, ALU.add))
                ffn_chain.settle()
                ffn_chain.did(dve.reciprocal(exp_inv[:, :], exp_sum[:, :]))
                ffn_chain.settle()
                ffn_chain.did(dve.tensor_tensor(prob[:, :].rearrange("p (a k) -> p a k", k=TOPK), expo[:, :, :],
                                            exp_inv[:, :].unsqueeze(2).broadcast_to([P, HEADS, TOPK]), ALU.mult))
                ffn_chain.settle()
                dve.wait_ge(idx_ready, n.t + 1)
                ffn_chain.did(dve.scalar_tensor_tensor(out=clamped[:, :], in0=idx[:, n.par, :], scalar=float(LAST),
                                                   in1=prob[:, :], op0=ALU.is_ge, op1=ALU.mult))
                ffn_chain.did(dve.scalar_tensor_tensor(out=pv[:, n.par, 1:SLOTS + 1], in0=idx[:, n.par, :],
                                                   scalar=float(LAST), in1=prob[:, :], op0=ALU.is_lt, op1=ALU.mult))
                ffn_chain.settle()
                ffn_chain.did(dve.tensor_reduce(pv[:, n.par, 0:1], clamped[:, :], AX_X, ALU.add))
                ffn_chain.settle()
                ffn_chain.end()

            def dot(c, s):
                g = s // GS
                if s % GS == 0:
                    need(dve, dots_ready, GROUPS * c.t + g - 1)
                    dve.wait_ge(gathered[g], 16 * GS * (c.t + 1))
                made = dve.tensor_tensor_reduce(products[:, s % (2 * GS), :], h[:, c.par, :], rows[:, s, 0:D], 1.0, 0.0, ALU.mult,
                                                ALU.add, dots[:, c.par, 1 + s:2 + s])
                if s % GS == GS - 1:
                    made.then_inc(dots_ready, 1)

            def weigh(c, g):
                a, b = (0 if g == 0 else 1 + GS * g), 1 + GS * (g + 1)
                dve.wait_ge(silu_ready, GROUPS * c.t + g + 1)
                dve.tensor_tensor(w[:, c.par, a:b], silu[:, c.par, a:b], pv[:, c.par, a:b],
                                  ALU.mult).then_inc(w_ready, 1)

            def mlp_gate(c, hf):
                n = 2 * c.t + hf + 1
                dve.wait_ge(up_ready, 2 * n)
                dve.wait_ge(mlp_silu_ready, n)
                need(dve, mt_ps_ready, n - 1)
                dve.tensor_tensor(mlp_m[:, :], mlp_silu[:, :], ps_u[:, :], ALU.mult).then_inc(m_ready, 1)

            def finish(c):
                dve.wait_ge(rows_used, GROUPS * (c.t + 1))
                dve.wait_ge(x1_copied, c.t + 1)
                dve.scalar_tensor_tensor(out=o_sb[:, c.par, :], in0=ps_acc[c.par][:, 0:D],
                                         scalar=gains[:, 1:2], in1=o_sb[:, c.par, :], op0=ALU.mult,
                                         op1=ALU.add).then_inc(out_ready, 1)

            first = tile_at(0, 0)
            norm_x(first)
            dve.wait_ge(gains_ready, 1)
            dve.wait_ge(cols_loaded, 16)
            dve.tensor_scalar(gain_gamma[:, :], cols_sb[:, 0:1], gains[:, 0:1], ATT_SCALE * CG, ALU.mult,
                              ALU.mult).then_inc(setup_dve, 1)
            dve.tensor_scalar(gain_beta[:, :], cols_sb[:, 1:2], gains[:, 0:1], None, ALU.mult).then_inc(setup_dve, 1)
            dve.wait_ge(setup_dve, 2)
            z_stats(first)
            pg_sums(first)
            spread(first)
            affine(first)
            dve.wait_ge(last_loaded, 16)
            residual(first)
            norm_h(first)
            key_tops0(first)
            key_tops1(first)
            pair_tops(first)
            dve.wait_ge(consts_loaded, 32)
            decode(first)
            weights(first)
            second = tile_at(0, 1)
            norm_x(second)
            z_stats(second)
            pg_sums(second)
            spread(second)
            affine(second)

            class Dots:

                def __init__(self, c):
                    self.c, self.s = c, 0

                def until(self, end):
                    while self.s < end:
                        dot(self.c, self.s)
                        self.s += 1

                def beside(self, chain, steps, n, end):
                    chain.beside = lambda: self.until(min(self.s + 1, end))
                    steps(n)
                    chain.beside = None

            def tile(c, before, after, after2):
                b, n, m = preceding(c), following(c), second_after(c)
                dots_c = Dots(c)
                if before:
                    mlp_gate(b, 1)
                if after:
                    residual(n)
                    norm_h(n)
                if after2:
                    dots_c.beside(attn_chain, norm_x, m, 8)
                dots_c.until(8)
                if before:
                    weigh(b, 6)
                dots_c.until(9)
                if after:
                    key_tops0(n)
                dots_c.until(12)
                if after:
                    key_tops1(n)
                if before:
                    weigh(b, 7)
                dots_c.until(13)
                if after:
                    pair_tops(n)
                weigh(c, 0)
                dots_c.until(14)
                weigh(c, 1)
                if after2:
                    z_stats(m)
                dots_c.until(15)
                if after:
                    decode(n)
                mlp_gate(c, 0)
                if before:
                    finish(b)
                if after2:
                    pg_sums(m)
                weigh(c, 2)
                dots_c.until(16)
                if after2:
                    spread(m)
                if after:
                    dots_c.beside(ffn_chain, weights, n, 24)
                dots_c.until(24)
                weigh(c, 3)
                if after2:
                    dots_c.beside(attn_chain, affine, m, 32)
                dots_c.until(32)
                weigh(c, 4)
                weigh(c, 5)

            def last_tile(c):
                b = preceding(c)
                dots_c = Dots(c)
                mlp_gate(b, 1)
                dots_c.until(GS)
                weigh(b, 6)
                weigh(b, 7)
                weigh(c, 0)
                dots_c.until(2 * GS)
                mlp_gate(c, 0)
                weigh(c, 1)
                dots_c.until(3 * GS)
                finish(b)
                weigh(c, 2)
                dots_c.until(4 * GS)
                mlp_gate(c, 1)
                weigh(c, 3)
                for g in range(4, GROUPS):
                    dots_c.until(GS * (g + 1))
                    weigh(c, g)
                finish(c)

            pipeline(tile, dve.Fori, last_tile)

        @block.scalar
        def _(act):
            act.dma_start(cols_sb[:, :], cols).then_inc(cols_loaded, 16)
            act.dma_start(consts_sb[:, :, :], consts).then_inc(consts_loaded, 16)
            act.dma_start(iota_sb[:, :], iota8).then_inc(consts_loaded, 16)

            def copy_g(n):
                act.wait_ge(gz_ready, n.t + 1)
                need(act, stats_ready, 2 * n.t)
                act.activation(g_copy[:, :], ps_gz[:, 0:D], ACT.Copy).then_inc(g_copied, 1)

            def scale_z(n):
                act.wait_ge(affine_ready, n.t + 1)
                need(act, h_ready, n.t)
                act.activation(att_out[:, :], ps_gz[:, D:2 * D], ACT.Copy, scale=sc[:, 23:24]).then_inc(att_ready, 1)

            def copy_ht(n):
                act.wait_ge(ht_ps_ready, n.t + 1)
                act.activation(h_t[:, n.par, :, :].rearrange("p k t -> p (k t)"), ps_p[:, 0:D],
                               ACT.Copy).then_inc(ht_ready, 1)

            def exps(n):
                act.wait_ge(shift_ready, n.t + 1)
                act.activation(expo[:, :, :], shifted[:, :, :], ACT.Exp).then_inc(exp_ready, 1)

            def silu_dots(c, g):
                a, b = (0 if g == 0 else 1 + GS * g), 1 + GS * (g + 1)
                act.wait_ge(dots_ready, GROUPS * c.t + g + 1)
                act.activation(silu[:, c.par, a:b], dots[:, c.par, a:b], ACT.Silu).then_inc(silu_ready, 1)

            def diags(c, g):
                act.wait_ge(w_ready, GROUPS * c.t + g + 1)
                need(act, rows_used, GROUPS * c.t + g + 1 - DIAGS)
                for j in range(0 if g == 0 else 1, GS + 1):
                    made = act.activation(diag[:, g % DIAGS, j, :], ident, ACT.Copy,
                                          scale=w[:, c.par, GS * g + j:GS * g + j + 1])
                made.then_inc(diag_ready, 1)

            def mlp_silu_of(c, hf):
                n = 2 * c.t + hf + 1
                act.wait_ge(up_ready, 2 * n - 1)
                need(act, m_ready, n - 1)
                act.activation(mlp_silu[:, :], ps_a[:, :], ACT.Silu).then_inc(mlp_silu_ready, 1)

            def copy_mt(c, hf):
                act.wait_ge(mt_ps_ready, 2 * c.t + hf + 1)
                act.activation(m_t[:, hf, :, :].rearrange("p k t -> p (k t)"), ps_t[:, :],
                               ACT.Copy).then_inc(mt_ready, 1)

            def copy_x1(c):
                act.wait_ge(h_ready, c.t + 1)
                need(act, stored, 16 * (c.t - 1))
                act.activation(o_sb[:, c.par, :], x1[:, c.par, :], ACT.Copy).then_inc(x1_copied, 1)

            first = tile_at(0, 0)
            act.wait_ge(cols_loaded, 16)
            act.activation(gains[:, :], cols_sb[:, 2:4], ACT.Tanh).then_inc(gains_ready, 1)
            act.wait_ge(wzt_ps_ready, 1)
            act.activation(wzt_sb[:, :], ps_acc[0][:, 0:P], ACT.Copy).then_inc(wzt_ready, 1)
            copy_g(first)
            wk_flat = wk_sb[:, :, :].rearrange("p k n -> p (k n)")

            def copy_wk(q, src):
                act.wait_ge(wk_ps_ready, q + 1)
                act.activation(wk_flat[:, 512 * q:512 * (q + 1)], src[:, :], ACT.Copy).then_inc(wk_ready, 1)

            copy_wk(0, ps_sim[0])
            scale_z(first)
            copy_wk(1, ps_sim[1])
            copy_wk(2, ps_a)
            copy_wk(3, ps_u)
            copy_ht(first)
            exps(first)
            act.wait_ge(consts_loaded, 32)
            copy_g(tile_at(0, 1))
            scale_z(tile_at(0, 1))

            def tile(c, before, after, after2):
                b, n, m = preceding(c), following(c), second_after(c)
                copy_x1(c)
                if before:
                    silu_dots(b, 6)
                    silu_dots(b, 7)
                    diags(b, 5)
                if after:
                    copy_ht(n)
                silu_dots(c, 0)
                if before:
                    copy_mt(b, 1)
                silu_dots(c, 1)
                if before:
                    diags(b, 6)
                mlp_silu_of(c, 0)
                if before:
                    diags(b, 7)
                if after2:
                    copy_g(m)
                diags(c, 0)
                silu_dots(c, 2)
                if after:
                    exps(n)
                diags(c, 1)
                diags(c, 2)
                copy_mt(c, 0)
                silu_dots(c, 3)
                mlp_silu_of(c, 1)
                diags(c, 3)
                silu_dots(c, 4)
                silu_dots(c, 5)
                if after2:
                    scale_z(m)
                diags(c, 4)

            def last_tile(c):
                b = preceding(c)
                copy_x1(c)
                silu_dots(b, 6)
                silu_dots(b, 7)
                diags(b, 5)
                copy_mt(b, 1)
                silu_dots(c, 0)
                mlp_silu_of(c, 0)
                diags(b, 6)
                diags(b, 7)
                silu_dots(c, 1)
                copy_mt(c, 0)
                diags(c, 0)
                diags(c, 1)
                silu_dots(c, 2)
                mlp_silu_of(c, 1)
                diags(c, 2)
                silu_dots(c, 3)
                diags(c, 3)
                copy_mt(c, 1)
                for g in range(4, GROUPS):
                    silu_dots(c, g)
                    diags(c, g)

            pipeline(tile, act.Fori, last_tile)

        @block.tensor
        def _(pe):
            def attn_gz(n):
                pe.wait_ge(x_loaded[n.par], 32 * (n.half + 1))
                need(pe, att_ready, n.t)
                pe.matmul(ps_gz[:, 0:D], wg_attn, ctx_sb[:, n.par, :], start=True, stop=True)
                pe.matmul(ps_gz[:, D:2 * D], wzt_sb[:, :], ctx_sb[:, n.par, :], start=True,
                          stop=True).then_inc(gz_ready, 1)

            def attn_p(n):
                pe.wait_ge(xn_ready, n.t + 1)
                need(pe, ht_ready, n.t)
                pe.matmul(ps_p[:, 0:D], wp_attn, xn[:, :], start=True, stop=True).then_inc(p_ready, 1)

            def group_means(n):
                pe.wait_ge(stats_ready, 2 * n.t + 2)
                pe.matmul(ps_p[:, STAT:STAT + 2], group_mean, rowstats[:, 0:2], start=True,
                          stop=True).then_inc(avg_ready, 1)

            def group_var(n):
                pe.wait_ge(q_ready, n.t + 1)
                pe.matmul(ps_p[:, STAT + 2:STAT + 3], group_mean, sc[:, 19:20], start=True,
                          stop=True).then_inc(avg_ready, 1)

            def turn_h(n):
                pe.wait_ge(h_ready, n.t + 1)
                for kt in range(KT):
                    last = pe.transpose(ps_p[:, P * kt:P * (kt + 1)], h[:, n.par, P * kt:P * (kt + 1)], ident)
                last.then_inc(ht_ps_ready, 1)

            def sims(n, f):
                if f == 0:
                    pe.wait_ge(ht_ready, n.t + 1)
                    need(pe, sims_used, n.t)
                for kt in range(KT):
                    last = pe.matmul(ps_sim[f][:, :], h_t[:, n.par, kt, :], wk_sb[:, kt, 512 * f:512 * (f + 1)],
                                     start=(kt == 0), stop=(kt == KT - 1))
                last.then_inc(sims_ready, 1)

            def mlp_up(c, hf, bank_, weights_):
                need(pe, mt_ready, 2 * c.t + hf)
                for kt in range(KT):
                    last = pe.matmul(bank_[:, :], h_t[:, c.par, kt, :], weights_[:, kt, HALF * hf:HALF * (hf + 1)],
                                     start=(kt == 0), stop=(kt == KT - 1))
                last.then_inc(up_ready, 1)

            def mlp_turn(c, hf):
                pe.wait_ge(m_ready, 2 * c.t + hf + 1)
                for q in range(HC):
                    turned = pe.transpose(ps_t[:, P * q:P * (q + 1)], mlp_m[:, P * q:P * (q + 1)], ident)
                turned.then_inc(mt_ps_ready, 1)

            def mlp_down(c, hf):
                pe.wait_ge(mt_ready, 2 * c.t + hf + 1)
                for q in range(HC):
                    pe.matmul(ps_acc[c.par][:, 0:D], m_t[:, hf, q, :], wd_sb[:, HC * hf + q, :],
                              start=False, stop=False)

            def experts(c, g):
                pe.wait_ge(diag_ready, GROUPS * c.t + g + 1)
                if g == 0:
                    need(pe, out_ready, c.t - 1)
                for j in range(0 if g == 0 else 1, GS + 1):
                    s = GS * g + j
                    up = last_sb[:, D:2 * D] if s == 0 else rows[:, s - 1, D:2 * D]
                    last = pe.matmul(ps_acc[c.par][:, 0:D], diag[:, g % DIAGS, j, :], up,
                                     start=(s == 0), stop=(s == SLOTS))
                last.then_inc(rows_used, 1)

            pe.wait_ge(attn_loaded, 16)
            pe.matmul(ps_acc[0][:, 0:P], wt_attn, wz_attn, start=True, stop=True).then_inc(wzt_ps_ready, 1)
            first = tile_at(0, 0)
            pe.wait_ge(wzt_ready, 1)
            attn_gz(first)
            attn_p(first)
            wk_banks = (ps_sim[0], ps_sim[1], ps_a, ps_u)
            wk_banks = (ps_sim[0], ps_sim[1], ps_a, ps_u)

            def fold_keys(kt):
                for ph in range(NH2):
                    at = NH2 * kt + ph
                    made = pe.matmul(wk_banks[at // 4][:, NKEYS * (at % 4):NKEYS * (at % 4 + 1)],
                                     wq_sb[:, ph, P * kt:P * (kt + 1)], keys_sb[:, ph, :], start=True, stop=True)
                    if at % 4 == 3:
                        made.then_inc(wk_ps_ready, 1)

            pe.wait_ge(consts_loaded, 32)
            group_means(first)
            group_var(first)
            pe.wait_ge(keys_loaded, 32)
            fold_keys(0)
            pe.wait_ge(affine_ready, 1)
            fold_keys(1)
            turn_h(first)
            pe.wait_ge(wk_ready, 4)
            sims(first, 0)
            sims(first, 1)
            second = tile_at(0, 1)
            attn_gz(second)
            attn_p(second)
            group_means(second)
            group_var(second)
            pe.wait_ge(mlp_loaded, 48)

            def tile(c, before, after, after2):
                b, n, m = preceding(c), following(c), second_after(c)
                if before:
                    mlp_turn(b, 1)
                if after:
                    turn_h(n)
                if before:
                    experts(b, 5)
                if after:
                    sims(n, 0)
                if after2:
                    attn_gz(m)
                if after:
                    sims(n, 1)
                mlp_up(c, 0, ps_a, wg_sb)
                if before:
                    experts(b, 6)
                    mlp_down(b, 1)
                if after2:
                    attn_p(m)
                if before:
                    experts(b, 7)
                mlp_up(c, 0, ps_u, wu_sb)
                experts(c, 0)
                if after2:
                    group_means(m)
                mlp_turn(c, 0)
                experts(c, 1)
                if after2:
                    group_var(m)
                mlp_up(c, 1, ps_a, wg_sb)
                experts(c, 2)
                mlp_up(c, 1, ps_u, wu_sb)
                experts(c, 3)
                mlp_down(c, 0)
                experts(c, 4)

            def last_tile(c):
                b = preceding(c)
                mlp_turn(b, 1)
                experts(b, 5)
                mlp_up(c, 0, ps_a, wg_sb)
                mlp_up(c, 0, ps_u, wu_sb)
                mlp_down(b, 1)
                experts(b, 6)
                mlp_turn(c, 0)
                experts(b, 7)
                experts(c, 0)
                mlp_up(c, 1, ps_a, wg_sb)
                mlp_up(c, 1, ps_u, wu_sb)
                experts(c, 1)
                mlp_down(c, 0)
                experts(c, 2)
                mlp_turn(c, 1)
                experts(c, 3)
                mlp_down(c, 1)
                for g in range(4, GROUPS):
                    experts(c, g)

            pipeline(tile, pe.Fori, last_tile)


def kernel(**inputs):
    import numpy as np
    import concourse.bacc as bacc
    from concourse import mybir as _mybir
    from concourse.bass_utils import run_bass_kernel_spmd

    a = {k: np.asarray(v) for k, v in inputs.items()}
    x = a["x"]
    b, c, d = x.shape
    heads, nkeys, _, kn = a["L0_ffn_keys"].shape
    inter = a["L0_ffn_Wg"].shape[0]
    kt = d // c
    cg = a["L0_xattn_Wz"].shape[1]
    table = np.concatenate([a["L0_ffn_down_embed"], a["L0_ffn_up_embed"]], axis=1)
    consts = np.zeros((c, 2, c), np.float32)
    consts[:, 0, :] = np.eye(c, dtype=np.float32)
    consts[:, 1, :] = np.kron(np.eye(c // cg, dtype=np.float32), np.full((cg, cg), 1.0 / cg, np.float32))
    wz_t = np.zeros((c, c), a["L0_xattn_Wz"].dtype)
    for g in range(c // cg):
        wz_t[cg * g:cg * g + cg, cg * g:cg * g + cg] = a["L0_xattn_Wz"][g].T
    laid = [
        ("x", x),
        ("ctx", a["ctx_1024"]),
        ("attn_w", np.stack([a["L0_xattn_Wp"].T, a["L0_xattn_Wg"].T, a["L0_xattn_Wt"], wz_t], axis=1)),
        ("cols", np.stack([a["L0_xattn_gamma"], a["L0_xattn_beta"],
                           np.broadcast_to(a["g_xattn"], (c,)), np.broadcast_to(a["g_ffn"], (c,))], axis=1)),
        ("wq", a["L0_ffn_Wq"].reshape(2 * heads, kn, d).transpose(1, 0, 2)),
        ("keys_t", a["L0_ffn_keys"].transpose(3, 2, 0, 1).reshape(kn, 2 * heads, nkeys)),
        ("table", table),
        ("last_row", np.broadcast_to(table[-1], (c, 2 * d))),
        ("wg_t", a["L0_ffn_Wg"].T.reshape(kt, c, inter).transpose(1, 0, 2)),
        ("wu_t", a["L0_ffn_Wu"].T.reshape(kt, c, inter).transpose(1, 0, 2)),
        ("wd_t", a["L0_ffn_Wd"].T.reshape(inter // c, c, d).transpose(1, 0, 2)),
        ("consts", consts),
        ("iota8", np.tile(np.arange(8, dtype=np.uint16), (c, 1))),
    ]
    nc = bacc.Bacc("TRN2", target_bir_lowering=False, num_devices=1)
    arrays, args = {}, []
    for name, value in laid:
        value = np.ascontiguousarray(value)
        arrays[f"in_{name}"] = value
        args.append(nc.dram_tensor(f"in_{name}", value.shape, _mybir.dt.from_np(value.dtype), kind="ExternalInput").ap())
    args.append(cg)
    args.append(nc.dram_tensor("out_y", x.shape, _mybir.dt.float32, kind="ExternalOutput").ap())
    gated_block(nc, *args)
    return run_bass_kernel_spmd(nc, [arrays], core_ids=[0]).results[0]["out_y"]
```
